# Optimizing a Trainium2 kernel written in Bass

```python
import numpy as np
import jax
import jax.numpy as jnp

def _softmax(x, axis=-1):
    return jax.nn.softmax(x, axis=axis)

def _gelu(x):
    return jax.nn.gelu(x, approximate=True)

def _silu(x):
    return jax.nn.silu(x)

def _sigmoid(x):
    return jax.nn.sigmoid(x)

def _layernorm(x, axis=-1, eps=1e-05):
    m = jnp.mean(x, axis=axis, keepdims=True)
    v = jnp.var(x, axis=axis, keepdims=True)
    return (x - m) / jnp.sqrt(v + eps)

def _scatter_add(tgt, idx, src, axis=0):
    return tgt.at[idx].add(src)

def _segment_sum(src, seg, n):
    return jax.ops.segment_sum(src, seg, n)
kernel_name = 'mk_flamingo_gated_d2_seqx_r8_b441f3'

def setup_inputs(seed: int=0):
    np.random.seed(seed)
    _w = jnp.asarray

    def _rec_inputs():
        import jax
        import jax.numpy as jnp
        _rk = jax.random.key(seed)
        x = 0.0002417 + 0.9998 * jax.random.normal(jax.random.fold_in(_rk, 1), (64, 128, 128), jnp.float32)
        _lenS = 128 - jax.random.randint(jax.random.fold_in(_rk, 7), (64,), 0, max(1, 128 // 4) + 1, jnp.int32)
        _lenS2 = 77 - jax.random.randint(jax.random.fold_in(_rk, 8), (64,), 0, max(1, 77 // 4) + 1, jnp.int32)
        _ctx_1024P = jax.random.normal(jax.random.fold_in(_rk, 11), (64, 16, 128), jnp.float32)
        _ctx_1024c = jax.random.dirichlet(jax.random.fold_in(_rk, 511), 0.3 * jnp.ones((16,), jnp.float32), (64, 77))
        _ctx_1024t = jnp.einsum('bsk,bkd->bsd', _ctx_1024c, _ctx_1024P)
        _ctx_1024t = _ctx_1024t * jax.lax.rsqrt(jnp.mean(jnp.square(_ctx_1024t)) + 1e-12) * 0.953939
        ctx_1024 = 7.22013e-05 + 1.00017 * (_ctx_1024t + 0.3 * jax.random.normal(jax.random.fold_in(_rk, 611), (64, 77, 128), jnp.float32))
        _validS = jnp.arange(128)[None, :] < _lenS[:, None]
        _validS2 = jnp.arange(77)[None, :] < _lenS2[:, None]
        _causal = jnp.tril(jnp.ones((128, 128), dtype=bool))
        mask_Bx1xSxS2_if1 = jnp.where(jnp.ones((64, 1, 128, 77), dtype=bool), 1, 0).astype(jnp.int32)
        mask_BxS2_ff1 = jnp.where(jnp.ones((64, 77), dtype=bool), 1.0, 0.0).astype(jnp.float32)
        _g = jax.random.normal(jax.random.fold_in(_rk, 9001), (2, 2), jnp.float32)
        _g = jnp.sign(_g) * jnp.maximum(jnp.abs(_g), 1.0) + (_g == 0) * 1.0
        g_xattn = _g[0]
        g_ffn = _g[1]
        return (x, ctx_1024, mask_Bx1xSxS2_if1, mask_BxS2_ff1, g_xattn, g_ffn)
    x, ctx_1024, mask_Bx1xSxS2_if1, mask_BxS2_ff1, g_xattn, g_ffn = _rec_inputs()

    def _L0_xattn_setup():
        import jax, jax.numpy as jnp
        import numpy as np
        EMBED = 128
        HEADS = 16
        HEAD_DIM = EMBED // HEADS
        key = jax.random.key(seed)
        ks = jax.random.split(key, 8)
        N, S = (4, 256)
        scale = 1.0 / np.sqrt(EMBED)
        return {'values': jax.random.normal(ks[0], (N, S, EMBED), jnp.float32), 'keys': jax.random.normal(ks[1], (N, S, EMBED), jnp.float32), 'query': jax.random.normal(ks[2], (N, S, EMBED), jnp.float32), 'mask': jnp.ones((N, 1, S, S), jnp.int32), 'Wv': jax.random.normal(ks[3], (EMBED, EMBED), jnp.float32) * scale, 'Wk': jax.random.normal(ks[4], (EMBED, EMBED), jnp.float32) * scale, 'Wq': jax.random.normal(ks[5], (EMBED, EMBED), jnp.float32) * scale, 'Wo': jax.random.normal(ks[6], (EMBED, EMBED), jnp.float32) * scale, 'bo': jnp.zeros((EMBED,), jnp.float32)}
    _L0_xattn_all = _L0_xattn_setup()
    _L0_xattn_in = {k: v for k, v in _L0_xattn_all.items() if k in ('Wv', 'Wk', 'Wq', 'Wo', 'bo')}
    del _L0_xattn_all

    def _L0_ffn_setup():
        import jax, jax.numpy as jnp
        import numpy as np
        B, S, D = (2, 512, 128)
        H = 512
        E = 8
        K = 4
        key = jax.random.key(seed)
        kx, kr, ku, kd = jax.random.split(key, 4)
        x = jax.random.normal(kx, (B, S, D), dtype=jnp.float32)
        router_w = jax.random.normal(kr, (D, E), dtype=jnp.float32) / np.sqrt(D)
        up_w = jax.random.normal(ku, (E, D, H), dtype=jnp.float32) / np.sqrt(D)
        down_w = jax.random.normal(kd, (E, H, D), dtype=jnp.float32) / np.sqrt(H)
        return {'x': x, 'router_w': router_w, 'up_w': up_w, 'down_w': down_w}
    _L0_ffn_all = _L0_ffn_setup()
    _L0_ffn_in = {k: v for k, v in _L0_ffn_all.items() if k in ('router_w', 'up_w', 'down_w')}
    del _L0_ffn_all

    def _L1_xattn_setup():
        import jax, jax.numpy as jnp
        import numpy as np
        MODEL_DIM = 128
        N_HEADS = 16
        HEAD_DIM = MODEL_DIM // N_HEADS
        BATCH = 2
        SEQ = 256

        def _split_heads(x):
            b, s, _ = x.shape
            return x.reshape(b, s, N_HEADS, HEAD_DIM).transpose(0, 2, 1, 3)
        key = jax.random.key(seed)
        ks = jax.random.split(key, 12)
        s = 1.0 / np.sqrt(MODEL_DIM)
        inp = {'k': jax.random.normal(ks[0], (BATCH, SEQ, MODEL_DIM), jnp.float32), 'q': jax.random.normal(ks[1], (BATCH, SEQ, MODEL_DIM), jnp.float32), 'v': jax.random.normal(ks[2], (BATCH, SEQ, MODEL_DIM), jnp.float32), 'attn_mask': jnp.ones((BATCH, SEQ), jnp.float32), 'Wq': jax.random.normal(ks[3], (MODEL_DIM, MODEL_DIM), jnp.float32) * s, 'bq': jax.random.normal(ks[4], (MODEL_DIM,), jnp.float32) * s, 'Wk': jax.random.normal(ks[5], (MODEL_DIM, MODEL_DIM), jnp.float32) * s, 'bk': jax.random.normal(ks[6], (MODEL_DIM,), jnp.float32) * s, 'Wv': jax.random.normal(ks[7], (MODEL_DIM, MODEL_DIM), jnp.float32) * s, 'bv': jax.random.normal(ks[8], (MODEL_DIM,), jnp.float32) * s, 'Wo': jax.random.normal(ks[9], (MODEL_DIM, MODEL_DIM), jnp.float32) * s, 'bo': jax.random.normal(ks[10], (MODEL_DIM,), jnp.float32) * s}
        return inp
    _L1_xattn_all = _L1_xattn_setup()
    _L1_xattn_in = {k: v for k, v in _L1_xattn_all.items() if k in ('Wq', 'bq', 'Wk', 'bk', 'Wv', 'bv', 'Wo', 'bo')}
    del _L1_xattn_all

    def _L1_ffn_setup():
        import jax, jax.numpy as jnp
        import numpy as np
        EMBED = 128
        D_FF = 4 * EMBED
        N_EXPERTS = 8
        TOP_K = 2
        B, S = (2, 128)
        key = jax.random.key(seed)
        ks = jax.random.split(key, 10)
        sc_d = 1.0 / np.sqrt(EMBED)
        sc_h = 1.0 / np.sqrt(D_FF)
        return {'inputs': jax.random.normal(ks[0], (B, S, EMBED), jnp.float32), 'rw1': jax.random.normal(ks[1], (EMBED, D_FF), jnp.float32) * sc_d, 'rb1': jnp.zeros((D_FF,), jnp.float32), 'rw2': jax.random.normal(ks[2], (D_FF, N_EXPERTS), jnp.float32) * sc_h, 'rb2': jnp.zeros((N_EXPERTS,), jnp.float32), 'W1': jax.random.normal(ks[3], (N_EXPERTS, EMBED, D_FF), jnp.float32) * sc_d, 'b1': jnp.zeros((N_EXPERTS, D_FF), jnp.float32), 'W2': jax.random.normal(ks[4], (N_EXPERTS, D_FF, EMBED), jnp.float32) * sc_h, 'b2': jnp.zeros((N_EXPERTS, EMBED), jnp.float32)}
    _L1_ffn_all = _L1_ffn_setup()
    _L1_ffn_in = {k: v for k, v in _L1_ffn_all.items() if k in ('rw1', 'rb1', 'rw2', 'rb2', 'W1', 'b1', 'W2', 'b2')}
    del _L1_ffn_all
    return {'x': x, 'ctx_1024': ctx_1024, 'mask_Bx1xSxS2_if1': mask_Bx1xSxS2_if1, 'mask_BxS2_ff1': mask_BxS2_ff1, 'g_xattn': g_xattn, 'g_ffn': g_ffn, 'L0_xattn_Wv': _L0_xattn_in['Wv'], 'L0_xattn_Wk': _L0_xattn_in['Wk'], 'L0_xattn_Wq': _L0_xattn_in['Wq'], 'L0_xattn_Wo': _L0_xattn_in['Wo'], 'L0_xattn_bo': _L0_xattn_in['bo'], 'L0_ffn_router_w': _L0_ffn_in['router_w'], 'L0_ffn_up_w': _L0_ffn_in['up_w'], 'L0_ffn_down_w': _L0_ffn_in['down_w'], 'L1_xattn_Wq': _L1_xattn_in['Wq'], 'L1_xattn_bq': _L1_xattn_in['bq'], 'L1_xattn_Wk': _L1_xattn_in['Wk'], 'L1_xattn_bk': _L1_xattn_in['bk'], 'L1_xattn_Wv': _L1_xattn_in['Wv'], 'L1_xattn_bv': _L1_xattn_in['bv'], 'L1_xattn_Wo': _L1_xattn_in['Wo'], 'L1_xattn_bo': _L1_xattn_in['bo'], 'L1_ffn_rw1': _L1_ffn_in['rw1'], 'L1_ffn_rb1': _L1_ffn_in['rb1'], 'L1_ffn_rw2': _L1_ffn_in['rw2'], 'L1_ffn_rb2': _L1_ffn_in['rb2'], 'L1_ffn_W1': _L1_ffn_in['W1'], 'L1_ffn_b1': _L1_ffn_in['b1'], 'L1_ffn_W2': _L1_ffn_in['W2'], 'L1_ffn_b2': _L1_ffn_in['b2']}

def reference(x, ctx_1024, mask_Bx1xSxS2_if1, mask_BxS2_ff1, g_xattn, g_ffn, L0_xattn_Wv, L0_xattn_Wk, L0_xattn_Wq, L0_xattn_Wo, L0_xattn_bo, L0_ffn_router_w, L0_ffn_up_w, L0_ffn_down_w, L1_xattn_Wq, L1_xattn_bq, L1_xattn_Wk, L1_xattn_bk, L1_xattn_Wv, L1_xattn_bv, L1_xattn_Wo, L1_xattn_bo, L1_ffn_rw1, L1_ffn_rb1, L1_ffn_rw2, L1_ffn_rb2, L1_ffn_W1, L1_ffn_b1, L1_ffn_W2, L1_ffn_b2):
    import jax
    import jax.numpy as jnp

    def _L0_xattn_ref(values, keys, query, mask, Wv, Wk, Wq, Wo, bo):
        import jax, jax.numpy as jnp
        import numpy as np
        EMBED = 128
        HEADS = 16
        HEAD_DIM = EMBED // HEADS
        N, Q = (query.shape[0], query.shape[1])
        K = keys.shape[1]
        v = (values @ Wv.T).reshape(N, K, HEADS, HEAD_DIM)
        k = (keys @ Wk.T).reshape(N, K, HEADS, HEAD_DIM)
        q = (query @ Wq.T).reshape(N, Q, HEADS, HEAD_DIM)
        att = jnp.einsum('nqhd,nkhd->nhqk', q, k)
        att = jnp.where(mask == 0, jnp.float32(-1e+20), att)
        att = jax.nn.softmax(att / np.sqrt(HEAD_DIM), axis=3)
        out = jnp.einsum('nhqk,nkhd->nqhd', att, v).reshape(N, Q, EMBED)
        return out @ Wo.T + bo

    def _L0_ffn_ref(x, router_w, up_w, down_w):
        import jax, jax.numpy as jnp
        import numpy as np
        B, S, D = (2, 512, 128)
        H = 512
        E = 8
        K = 4
        router_logits = jnp.einsum('bsd,de->bse', x, router_w)
        routing_weights = jax.nn.softmax(router_logits, axis=-1)
        topk_weights, topk_indices = jax.lax.top_k(routing_weights, K)
        topk_weights = topk_weights / jnp.sum(topk_weights, axis=-1, keepdims=True)
        h = jnp.einsum('bsd,edh->bseh', x, up_w)
        h = jax.nn.gelu(h)
        expert_outputs = jnp.einsum('bseh,ehd->bsed', h, down_w)
        gathered = jnp.take_along_axis(expert_outputs, topk_indices[:, :, :, None], axis=2)
        output = jnp.sum(topk_weights[:, :, :, None] * gathered, axis=2)
        return output

    def _L1_xattn_ref(k, q, v, attn_mask, Wq, bq, Wk, bk, Wv, bv, Wo, bo):
        import jax, jax.numpy as jnp
        import numpy as np
        MODEL_DIM = 128
        N_HEADS = 16
        HEAD_DIM = MODEL_DIM // N_HEADS
        BATCH = 2
        SEQ = 256

        def _split_heads(x):
            b, s, _ = x.shape
            return x.reshape(b, s, N_HEADS, HEAD_DIM).transpose(0, 2, 1, 3)
        kh = _split_heads(k @ Wk.T + bk)
        qh = _split_heads(q @ Wq.T + bq)
        vh = _split_heads(v @ Wv.T + bv)
        scores = jnp.einsum('bhqd,bhkd->bhqk', qh, kh) / jnp.sqrt(jnp.asarray(HEAD_DIM, qh.dtype))
        neg = jnp.finfo(scores.dtype).min
        mask = attn_mask[:, None, None, :]
        scores = scores + (1.0 - mask) * neg
        weights = jax.nn.softmax(scores, axis=-1)
        attn = jnp.einsum('bhqk,bhkd->bhqd', weights, vh)
        b, h, s, d = attn.shape
        attn = attn.transpose(0, 2, 1, 3).reshape(b, s, h * d)
        return attn @ Wo.T + bo

    def _L1_ffn_ref(inputs, rw1, rb1, rw2, rb2, W1, b1, W2, b2):
        import jax, jax.numpy as jnp
        import numpy as np
        EMBED = 128
        D_FF = 4 * EMBED
        N_EXPERTS = 8
        TOP_K = 2
        B, S = (2, 128)
        Bb, Ss, D = inputs.shape
        T = Bb * Ss
        xf = inputs.reshape(T, D)
        score = jax.nn.relu(xf @ rw1 + rb1) @ rw2 + rb2
        _, topi = jax.lax.top_k(score, TOP_K)
        mask = jnp.zeros(score.shape, bool).at[jnp.arange(T)[:, None], topi].set(True)
        gate = jax.nn.softmax(jnp.where(mask, score, -jnp.inf), axis=-1)
        out = jnp.zeros_like(xf)
        for e in range(N_EXPERTS):
            h = jax.nn.relu(xf @ W1[e] + b1[e])
            y = h @ W2[e] + b2[e]
            out = out + gate[:, e:e + 1] * y
        return out.reshape(Bb, Ss, D)
    x = x + jnp.tanh(g_xattn[0]) * _L0_xattn_ref(ctx_1024, ctx_1024, _layernorm(x, axis=-1), mask_Bx1xSxS2_if1, L0_xattn_Wv, L0_xattn_Wk, L0_xattn_Wq, L0_xattn_Wo, L0_xattn_bo)
    x = x + jnp.tanh(g_ffn[0]) * _L0_ffn_ref(_layernorm(x, axis=-1), L0_ffn_router_w, L0_ffn_up_w, L0_ffn_down_w)
    x = x + jnp.tanh(g_xattn[1]) * _L1_xattn_ref(ctx_1024, _layernorm(x, axis=-1), ctx_1024, mask_BxS2_ff1, L1_xattn_Wq, L1_xattn_bq, L1_xattn_Wk, L1_xattn_bk, L1_xattn_Wv, L1_xattn_bv, L1_xattn_Wo, L1_xattn_bo)
    x = x + jnp.tanh(g_ffn[1]) * _L1_ffn_ref(_layernorm(x, axis=-1), L1_ffn_rw1, L1_ffn_rb1, L1_ffn_rw2, L1_ffn_rb2, L1_ffn_W1, L1_ffn_b1, L1_ffn_W2, L1_ffn_b2)
    return x

_drawn_inputs = setup_inputs


def setup_inputs(seed=0):
    import zlib

    import numpy as np

    out = dict(_drawn_inputs(seed))
    spreads = {'g_ffn': (-1.0, 0.574),
     'L0_xattn_bo': (0.0, 0.1),
     'L1_ffn_rb1': (0.0, 0.1),
     'L1_ffn_rb2': (0.0, 0.1),
     'L1_ffn_b1': (0.0, 0.1),
     'L1_ffn_b2': (0.0, 0.1)}
    factors = {'L1_xattn_bk': 8.0}
    for name, (base, spread) in spreads.items():
        noise = np.random.default_rng([zlib.crc32(name.encode()), seed]).standard_normal(out[name].shape)
        drawn = base * np.exp(spread * noise) if base else spread * noise
        out[name] = jnp.asarray(drawn.astype(out[name].dtype))
    for name, factor in factors.items():
        out[name] = (out[name] * factor).astype(out[name].dtype)
    return out
```

```python
from contextlib import ExitStack

import numpy as np

import concourse.bass as bass
from concourse import mybir

F32 = mybir.dt.float32
F16 = mybir.dt.float16
BF16 = mybir.dt.bfloat16
I32 = mybir.dt.int32
ALU = mybir.AluOpType
ACT = mybir.ActivationFunctionType
AX = mybir.AxisListType.X

B, S, D = 64, 128, 128
K2 = 77
H, HD = 16, 8
G = 4
E, HID = 8, 512
C = HID // 128
TB = 4
NBLK = B // TB
TOK = TB * S
TOPK = (4, 2)
INV = 1.0 / np.sqrt(np.float32(HD))
PEN0 = float(-1e20 * INV)
FMIN = float(np.finfo(np.float32).min)
EPS = 1e-5

BQ, BK, BV, BO1, BO0, B2, RB2 = 0, 512, 1024, 1152, 1280, 1408, 1408 + E * D
NBIAS = RB2 + E
C_ID, C_NQ, C_NK, C_SEL, C_UP, C_LOW, C_HALF, C_EPS = 0, 128, 129, 130, 133, 197, 261, 265
NCONST = C_EPS + TB


def wait(eng, sem, value):
    if isinstance(value, int) and value <= 0:
        return
    eng.wait_ge(sem, value)


def loaded(i, p):
    return 8 * (i - p) + 16


def flamingo(nc, x, ctx_in, mask0, mask1, gates_in, consts, wq, wk, wv, wo, biases, rw0, up, down, rw1, rw2, b1, rb1, out):
    with ExitStack() as ctx:
        def sb(name, shape, dt):
            return ctx.enter_context(nc.sbuf_tensor(name, shape, dt))

        def sem(name):
            return ctx.enter_context(nc.semaphore(name))

        made = {}

        def shared_sem(name):
            if name not in made:
                made[name] = sem(name)
            return made[name]

        x_all = sb("x_all", [128, B, D], F32)
        cst = sb("cst", [128, NCONST], F32)
        ident_bf = sb("ident_bf", [128, 128], BF16)
        ones_all = sb("ones_all", [128, 128], BF16)
        ones_bf = ones_all[0:3, :]
        tg = sb("tg", [128, 4], F32)
        wq_s = sb("wq_s", [128, 2, G, 128], F32)
        wk_s = sb("wk_s", [128, 2, G, 128], F32)
        wv_s = sb("wv_s", [128, 2, 128], F32)
        wo_s = sb("wo_s", [128, 2, 128], F32)
        bias_bf = sb("bias_bf", [3, NBIAS], BF16)
        pen_f = sb("pen_f", [B, 4, K2], F32)
        pen_parts = sb("pen_parts", [B, 3, K2], BF16)
        pen1 = sb("pen1", [128, B, K2], BF16)
        stage = sb("stage", [128, E, HID], F32)
        up_hl = sb("up_hl", [128, 2, E, HID], F16)
        down_hl = sb("down_hl", [128, 2, E, C, D], F16)
        small_w = sb("small_w", [128, E + HID + C * E + E * C + C], F32)
        rw0_hl = sb("rw0_hl", [128, 2, E], F16)
        rw1_hl = sb("rw1_hl", [128, 2, HID], F16)
        rw2_hl = sb("rw2_hl", [128, 2, C, E], F16)
        ctx_s = sb("ctx_s", [K2, 2, D], F32)
        mask_s = sb("mask_s", [128, 2, K2], I32)
        pen0 = sb("pen0", [128, 2, K2], BF16)
        stats = sb("stats", [128, 2, 6], F32)
        mv = sb("mv", [128, 2, 2], F32)
        rstd = sb("rstd", [128, 2, 1], F32)
        xn = sb("xn", [128, 2, D], F32)
        xc_t = sb("xc_t", [128, 2, 128 + K2], F32)
        q_hi = sb("q_hi", [128, G, 128], F16)
        q_st = sb("q_st", [128, 2, G, 128], F16)
        k_hi = sb("k_hi", [128, G, K2], F16)
        k_st = sb("k_st", [128, 2, G, K2], F16)
        v_s = sb("v_s", [K2, 2, H, 32], F32)
        mx = sb("mx", [128, H], F32)
        sd = sb("sd", [128, 4, G, K2], F32)
        NP, NPT = 2 * H * K2, H * 128
        shared = sb("shared", [128, NP + NPT], F32)
        p_s = shared[:, 0:NP].rearrange("q (a j g k) -> q a j g k", a=2, j=4, g=G)
        pt_s = shared[0:K2, NP:NP + NPT].rearrange("k (j g q) -> k j g q", j=4, g=G)
        u_s = sb("u_s", [128, 2, G, 128], F32)
        rden = sb("rden", [128, H], F32)
        an = sb("an", [128, H, HD], F32)
        at = sb("at", [128, 128], F32)
        xn4 = sb("xn4", [128, 2, TB, D], F32)
        wide = sb("wide", [128, B * S], F32)
        xt_hl = wide[:, :].bitcast(F16).rearrange("p (a n) -> p a n", a=2)
        bias_f = wide[0:3, 0:3 * NBIAS].rearrange("p (a n) -> p a n", a=3)
        h32 = sb("h32", [128, C, TOK], F32)
        h_hl = shared[:, 0:2 * C * TOK].bitcast(F16).rearrange("p (a t c n) -> p a t c n", a=2, t=2, c=C)
        lg = sb("lg", [128, TB, E], F32)
        cmp_a = sb("cmp_a", [128, TB, E, E], F32)
        cmp_b = sb("cmp_b", [128, TB, E, E], F32)
        rank = sb("rank", [128, TB, E], F32)
        lmax = sb("lmax", [128, TB], F32)
        lsum = sb("lsum", [128, TB], F32)
        gate = sb("gate", [128, B, E], F32)

        ps_s = ctx.enter_context(nc.psum_tensor("ps_s", [128, 4, 512], F32))
        ps_a = ctx.enter_context(nc.psum_tensor("ps_a", [128, 512], F32))
        ps_b = ctx.enter_context(nc.psum_tensor("ps_b", [128, 512], F32))
        ps_6 = ctx.enter_context(nc.psum_tensor("ps_6", [128, 512], F32))
        ps_7 = ctx.enter_context(nc.psum_tensor("ps_7", [128, 512], F32))

        ident = cst[:, C_ID:C_ID + 128]

        names = ("setup_ld", "w_ld", "pen_ld", "const_ok", "bias_ok", "split_ok", "pen_moved", "rsplit_ok",
                 "phase_end", "setup_chain", "out_st")
        m = {n: sem(n) for n in names}
        block = ctx.enter_context(nc.Block())
        progs = {k: [] for k in ("sp", "act", "dve", "pool", "pe")}

        def setup_sp(sp):
            sp.dma_start(cst[:, :], consts).then_inc(m["setup_ld"], 16)
            sp.dma_start(tg[:, :], gates_in.partition_broadcast(128)).then_inc(m["setup_ld"], 16)
            sp.dma_start(wq_s[:, :, :, :], wq).then_inc(m["setup_ld"], 16)
            sp.dma_start(wk_s[:, :, :, :], wk).then_inc(m["setup_ld"], 16)
            sp.dma_start(wv_s[:, :, :], wv).then_inc(m["setup_ld"], 16)
            sp.dma_start(wo_s[:, :, :], wo).then_inc(m["setup_ld"], 16)
            sp.dma_start(bias_f[:, 0, :], biases).then_inc(m["setup_ld"], 16)
            sp.dma_start(pen_f[:, 0, :], mask1).then_inc(m["setup_ld"], 16)
            sp.dma_start(small_w[:, :], rw_all).then_inc(m["setup_ld"], 16)

        NLD = 16 * 9
        rw_all = rw0
        o = 0
        rw0_f = small_w[:, o:o + E]; o += E
        rw1_f = small_w[:, o:o + HID]; o += HID
        rw2_f = small_w[:, o:o + C * E].rearrange("p (c e) -> p c e", c=C); o += C * E
        b1_f = small_w[:, o:o + E * C].rearrange("p (e c) -> p e c", e=E); o += E * C
        rb1_f = small_w[:, o:o + C]

        def setup_pool(pool):
            nc.gpsimd.memset(v_s[:, :, :, :], 0.0).then_inc(m["setup_chain"], 1)
            nc.gpsimd.memset(ones_all[:, :], 0.0).then_inc(m["setup_chain"], 1)
            nc.gpsimd.memset(pen1[:, :, :], 0.0).then_inc(m["const_ok"], 1)
            pool.wait_ge(m["setup_chain"], 2)
            nc.gpsimd.memset(ones_bf[:, :], 1.0).then_inc(m["const_ok"], 1)
            nc.gpsimd.memset(v_s[:, :, :, HD:HD + 1], 1.0).then_inc(m["const_ok"], 1)
            pool.wait_ge(m["setup_ld"], NLD)
            nc.gpsimd.tensor_copy(ident_bf[:, :], ident).then_inc(m["const_ok"], 1)

        def setup_act(act):
            act.wait_ge(m["setup_ld"], NLD)
            nc.scalar.activation(tg[:, :], tg[:, :], ACT.Tanh).then_inc(m["const_ok"], 1)

        def parts(dve, v, chain):
            mask = -65536
            for k in range(1, 3):
                chain(nc.vector.tensor_single_scalar(v[:, k].bitcast(I32), v[:, 0].bitcast(I32), mask, op=ALU.bitwise_and))
                chain(nc.vector.tensor_tensor(v[:, 0], v[:, 0], v[:, k], ALU.subtract))
            chain(nc.vector.tensor_copy(v[:, 3], v[:, 0]))

        def setup_dve(dve):
            count = [0]
            chain_sem = m["bias_ok"]

            def chain(ins):
                count[0] += 1
                ins.then_inc(chain_sem, 1)
                dve.wait_ge(chain_sem, count[0])

            dve.wait_ge(m["setup_ld"], NLD)
            nc.vector.tensor_scalar(wq_s[:, :, :, :], wq_s[:, :, :, :], float(INV), None, ALU.mult).then_inc(m["const_ok"], 1)
            v, part, kept = bias_f[:, 0], bias_f[:, 1], bias_f[:, 2]
            sel = cst[0:3, C_SEL:C_SEL + 3]
            chain(nc.vector.tensor_scalar(v[:, BQ:BQ + 512], v[:, BQ:BQ + 512], float(INV), None, ALU.mult))
            chain(nc.vector.tensor_single_scalar(part.bitcast(I32), v.bitcast(I32), -65536, op=ALU.bitwise_and))
            chain(nc.vector.tensor_tensor(v, v, part, ALU.subtract))
            chain(nc.vector.tensor_scalar(kept, part, sel[:, 0:1], None, ALU.mult))
            chain(nc.vector.tensor_single_scalar(part.bitcast(I32), v.bitcast(I32), -65536, op=ALU.bitwise_and))
            chain(nc.vector.tensor_tensor(v, v, part, ALU.subtract))
            chain(nc.vector.scalar_tensor_tensor(kept, part, sel[:, 1:2], kept, ALU.mult, ALU.add))
            chain(nc.vector.scalar_tensor_tensor(bias_bf[:, :], v, sel[:, 2:3], kept, ALU.mult, ALU.add))
            chain(nc.vector.tensor_scalar(pen_f[:, 0, :], pen_f[:, 0, :], -1.0, 1.0, ALU.mult, ALU.add))
            chain(nc.vector.tensor_scalar(pen_f[:, 0, :], pen_f[:, 0, :], FMIN, None, ALU.mult))
            parts(dve, pen_f, chain)
            chain(nc.vector.tensor_copy(pen_parts[:, :, :], pen_f[:, 1:4, :]))
            for k, (hl, w) in enumerate(((rw0_hl, rw0_f), (rw1_hl, rw1_f), (rw2_hl, rw2_f))):
                chain(nc.vector.tensor_copy(hl[:, 0], w))
                chain(nc.vector.tensor_tensor(hl[:, 1], w, hl[:, 0], ALU.subtract))
            assert count[0] == BIAS_STEPS

        BIAS_STEPS = 8 + 2 + 5 + 1 + 6
        NCONST_OK = 6

        def pen_sp(sp):
            sp.wait_ge(m["bias_ok"], BIAS_STEPS)
            sp.wait_ge(m["const_ok"], NCONST_OK)
            for k in range(3):
                sp.dma_start(pen1[k:k + 1, :, :], pen_parts[:, k, :]).then_inc(m["pen_moved"], 16)

        def attention(layer):
            o = layer * B
            n = ("x_ld0", "x_ld1", "ctx_ld0", "ctx_ld1", "mask_ld0", "mask_ld1", "pen", "st1", "st2", "st3", "st4", "xn", "xct", "xct_ev", "q", "q_hi", "q_st",
                 "kv", "v_ev", "k_hi", "k_st", "s", "mx", "sd", "p", "pt0", "pt1", "pt2", "pt3", "pe0", "pe1", "pe2", "pe3",
                 "u", "u_ev", "ut", "rden", "an", "a_t", "at_ev", "o", "x_new")
            s = {k: shared_sem("a_" + k) for k in n}
            neg_q, neg_k = cst[:, C_NQ:C_NQ + 1], cst[:, C_NK:C_NK + 1]

            def load(sp, i, p):
                if layer == 0:
                    wait(sp, s["st1"], i - 1)
                    sp.dma_start(x_all[:, bass.ds(i - o, 1), :], x[bass.ds(i - o, 1), :, :].rearrange("b s d -> s b d")).then_inc(s[f"x_ld{p}"], 16)
                wait(sp, s["xct"], i - 1)
                sp.dma_start(ctx_s[:, p, :], ctx_in[bass.ds(i - o, 1), :, :].rearrange("b s d -> s (b d)")).then_inc(s[f"ctx_ld{p}"], 16)
                if layer == 0:
                    wait(sp, s["pen"], i - 1)
                    sp.dma_start(mask_s[:, p, :], mask0[bass.ds(i - o, 1), 0, :, :].rearrange("b s k -> s (b k)")).then_inc(s[f"mask_ld{p}"], 16)

            def sp_prog(sp):
                if layer == 0:
                    setup_sp(sp)
                else:
                    sp.wait_ge(m["phase_end"], 3 * 4)
                load(sp, o, 0)
                load(sp, o + 1, 1)
                if layer == 0:
                    pen_sp(sp)
                with sp.Fori(o + 2, o + B - 1, 2) as i:
                    load(sp, i, 0)
                    load(sp, i + 1, 1)

            def pool_batch(pool, i, p):
                if layer == 0:
                    wait(pool, s[f"mask_ld{p}"], loaded(i, p))
                    wait(pool, s["s"], i - 1)
                wait(pool, s["st2"], i + 1)
                nc.gpsimd.tensor_tensor(rstd[:, p, :], mv[:, p, 1:2], cst[:, C_EPS:C_EPS + 1], ALU.add).then_inc(s["st3"], 1)
                if layer == 0:
                    nc.gpsimd.tensor_scalar(pen0[:, p, :], mask_s[:, p, :], 0, PEN0, ALU.is_equal, ALU.mult).then_inc(s["pen"], 1)
                wait(pool, s["st3"], i + 1)
                nc.gpsimd.tensor_tensor(rstd[:, p, :], rstd[:, p, :], cst[:, C_HALF:C_HALF + 1], ALU.pow).then_inc(s["st4"], 1)

            def pool_prog(pool):
                if layer == 0:
                    setup_pool(pool)
                pool_batch(pool, o, 0)
                pool_batch(pool, o + 1, 1)
                with pool.Fori(o + 2, o + B - 1, 2) as i:
                    pool_batch(pool, i, 0)
                    pool_batch(pool, i + 1, 1)
                phase_end(pool)

            def front(pe, i, p, mid, tail, prev):
                q = 1 - p
                if front_on(i):
                    pe.wait_ge(s["xn"], i + 1)
                    pe.wait_ge(s[f"ctx_ld{p}"], loaded(i, p))
                    wait(pe, s["k_st"], i)
                    nc.tensor.transpose(ps_6[:, 0:128], xn[:, p, :], ident)
                    nc.tensor.transpose(ps_6[:, 128:128 + K2], ctx_s[:, p, :], ident[0:K2, 0:K2]).then_inc(s["xct"], 1)
                if tail:
                    t = i - 2
                    pe.wait_ge(s["u_ev"], t + 1)
                    wait(pe, s["x_new"], t)
                    for g in range(G):
                        mm = nc.tensor.transpose(ps_7[:, g * 128:(g + 1) * 128], u_s[:, p, g, :], ident)
                    mm.then_inc(s["ut"], 1)
                if front_on(i):
                    pe.wait_ge(s["xct_ev"], i + 1)
                    for g in range(G):
                        o_ = ps_6[:, g * 128:(g + 1) * 128]
                        mm = nc.tensor.matmul(o_, wq_s[:, layer, g, :], xc_t[:, p, 0:128], start=True, stop=layer == 0)
                        if layer:
                            mm = nc.tensor.matmul(o_, bias_bf[:, BQ + g * 128:BQ + (g + 1) * 128], ones_bf[:, :], start=False, stop=True)
                    mm.then_inc(s["q"], 1)
                if tail:
                    pe.wait_ge(s["an"], t + 1)
                    nc.tensor.transpose(ps_7[:, 0:128], an[:, :, :].rearrange("q h d -> q (h d)"), ident).then_inc(s["a_t"], 1)
                if front_on(i):
                    pe.wait_ge(s["q_st"], i + 1)
                    for g in range(G):
                        o_ = ps_6[:, g * K2:(g + 1) * K2]
                        nc.tensor.matmul(o_, wk_s[:, layer, g, :], xc_t[:, p, 128:128 + K2], start=True, stop=layer == 0)
                        if layer:
                            nc.tensor.matmul(o_, bias_bf[:, BK + g * 128:BK + (g + 1) * 128], ones_bf[:, 0:K2], start=False, stop=True)
                    o_ = ps_6[0:K2, G * K2:G * K2 + 128]
                    mm = nc.tensor.matmul(o_, xc_t[:, p, 128:128 + K2], wv_s[:, layer, :], start=True, stop=layer == 0)
                    if layer:
                        mm = nc.tensor.matmul(o_, ones_bf[:, 0:K2], bias_bf[:, BV:BV + 128], start=False, stop=True)
                    mm.then_inc(s["kv"], 1)
                if tail:
                    pe.wait_ge(s["at_ev"], t + 1)
                    nc.tensor.matmul(ps_7[:, 0:128], at[:, :], wo_s[:, layer, :], start=True, stop=False)
                    bo = BO1 if layer else BO0
                    nc.tensor.matmul(ps_7[:, 0:128], ones_bf[:, :], bias_bf[:, bo:bo + 128], start=False, stop=True).then_inc(s["o"], 1)
                if mid:
                    k = i - 1
                    pe.wait_ge(s["p"], k + 1)
                    wait(pe, s["u_ev"], k)
                    for j in (0, 1):
                        ps = (ps_a, ps_b)[j % 2]
                        if j == 1:
                            wait(pe, s["pe3"], k)
                        for g in range(G):
                            mm = nc.tensor.transpose(ps[0:K2, g * 128:(g + 1) * 128], p_s[:, q, j, g, :], ident)
                        mm.then_inc(s[f"pt{j}"], 1)
                if front_on(i):
                    pe.wait_ge(s["k_st"], i + 1)
                    if layer == 0:
                        pe.wait_ge(s["pen"], i + 1)
                    wait(pe, s["sd"], i)
                    for j in range(4):
                        o_ = ps_s[:, j, 0:G * K2].rearrange("q (g k) -> q g k", g=G)
                        if layer == 0:
                            nc.tensor.matmul(o_, ident_bf[:, :], pen0[:, p:p + 1, :].broadcast_to([128, G, K2]), start=True, stop=True)
                        else:
                            nc.tensor.matmul(o_, ones_all[:, :], pen1[:, bass.ds(i - o, 1), :].broadcast_to([128, G, K2]), start=True, stop=True)
                    for g in range(G):
                        for j in range(4):
                            r = 32 * j
                            mm = nc.tensor.matmul(ps_s[:, j, g * K2:(g + 1) * K2], q_st[r:r + 32, p, g, :], k_st[r:r + 32, p, g, :],
                                                  start=False, stop=True, skip_group_check=True)
                    mm.then_inc(s["s"], 1)
                if mid:
                    for j in (2, 3):
                        ps = (ps_a, ps_b)[j % 2]
                        pe.wait_ge(s[f"pe{j - 2}"], k + 1)
                        for g in range(G):
                            mm = nc.tensor.transpose(ps[0:K2, g * 128:(g + 1) * 128], p_s[:, q, j, g, :], ident)
                        mm.then_inc(s[f"pt{j}"], 1)
                    pe.wait_ge(s["pe2"], k + 1)
                    pe.wait_ge(s["pe3"], k + 1)
                    for g in range(G):
                        for j in range(4):
                            mm = nc.tensor.matmul(ps_a[32 * j:32 * j + 32, g * 128:(g + 1) * 128], v_s[:, q, 4 * g + j, :],
                                                  pt_s[:, j, g, :], start=True, stop=True)
                    mm.then_inc(s["u"], 1)

            def front_on(i):
                return not isinstance(i, int) or i < o + B

            def steps(eng, f):
                f(eng, o, 0, False, False, None)
                f(eng, o + 1, 1, True, False, None)
                with eng.Fori(o + 2, o + B - 1, 2) as i:
                    f(eng, i, 0, True, True, None)
                    f(eng, i + 1, 1, True, True, None)
                f(eng, o + B, 0, True, True, None)
                f(eng, o + B + 1, 1, False, True, None)

            def pe_prog(pe):
                if layer == 0:
                    pe.wait_ge(m["setup_ld"], NLD)
                    pe.wait_ge(m["const_ok"], NCONST_OK)
                    pe.wait_ge(m["bias_ok"], BIAS_STEPS)
                else:
                    pe.wait_ge(m["pen_moved"], 48)
                    pe.wait_ge(m["phase_end"], 3 * 4)
                steps(pe, front)
                phase_end(pe)

            def act_batch(act, i, p, mid, tail, _):
                q = 1 - p
                if front_on(i):
                    act.wait_ge(s["xct"], i + 1)
                    wait(act, s["kv"], i - 1)
                    nc.scalar.activation(xc_t[:, p, :], ps_6[:, 0:128 + K2], ACT.Copy).then_inc(s["xct_ev"], 1)
                    act.wait_ge(s["q"], i + 1)
                    wait(act, s["q_st"], i)
                    nc.scalar.activation(q_hi[:, :, :].rearrange("p g q -> p (g q)"), ps_6[:, :], ACT.Copy).then_inc(s["q_hi"], 1)
                if tail:
                    act.wait_ge(s["a_t"], i - 1)
                    wait(act, s["o"], i - 2)
                    nc.scalar.activation(at[:, :], ps_7[:, 0:128], ACT.Copy).then_inc(s["at_ev"], 1)
                if front_on(i):
                    act.wait_ge(s["kv"], i + 1)
                    wait(act, s["u"], i - 1)
                    nc.scalar.activation(v_s[:, p, :, 0:HD], ps_6[0:K2, G * K2:G * K2 + 128].rearrange("k (h d) -> k h d", h=H),
                                         ACT.Copy).then_inc(s["v_ev"], 1)
                    wait(act, s["k_st"], i)
                    nc.scalar.activation(k_hi[:, :, :].rearrange("p g k -> p (g k)"), ps_6[:, 0:G * K2], ACT.Copy).then_inc(s["k_hi"], 1)
                if mid:
                    k = i - 1
                    for j in (1, 2, 3):
                        act.wait_ge(s[f"pt{j}"], k + 1)
                        if j == 1:
                            wait(act, s["u"], k)
                        ps = (ps_a, ps_b)[j % 2]
                        nc.scalar.activation(pt_s[:, j, :, :].rearrange("k g q -> k (g q)"), ps[0:K2, :], ACT.Copy).then_inc(s[f"pe{j}"], 1)
                    act.wait_ge(s["u"], k + 1)
                    wait(act, s["ut"], k - 1)
                    nc.scalar.activation(u_s[:, q, :, :].rearrange("p g q -> p (g q)"), ps_a[:, :], ACT.Copy).then_inc(s["u_ev"], 1)
                if front_on(i):
                    act.wait_ge(s["sd"], i + 1)
                    wait(act, s["pt3"], i - 1)
                    nc.scalar.activation(p_s[:, p].rearrange("q j g k -> q (j g k)"), sd[:, :, :, :].rearrange("q j g k -> q (j g k)"),
                                         ACT.Exp).then_inc(s["p"], 1)

            def act_prog(act):
                if layer == 0:
                    setup_act(act)
                    act.wait_ge(m["const_ok"], NCONST_OK)
                else:
                    act.wait_ge(m["phase_end"], 3 * 4)
                steps(act, act_batch)
                phase_end(act)

            def norm_stats(dve, i, p):
                xb = x_all[:, bass.ds(i - o, 1), :].rearrange("s b d -> s (b d)")
                if layer == 0:
                    wait(dve, s[f"x_ld{p}"], loaded(i, p))
                wait(dve, s["xn"], i - 1)
                nc.vector.bn_stats(stats[:, p, :], xb).then_inc(s["st1"], 1)

            def norm_aggregate(p):
                nc.vector.bn_aggr(mv[:, p, :], stats[:, p, :]).then_inc(s["st2"], 1)

            def normalise(dve, i, p, n):
                wait(dve, s["st1"], n)
                wait(dve, s["st4"], i + 1)
                wait(dve, s["xct"], i - 1)
                nc.vector.tensor_scalar(xn[:, p, :], x_all[:, bass.ds(i - o, 1), :].rearrange("s b d -> s (b d)"), mv[:, p, 0:1], rstd[:, p, :],
                                        ALU.subtract, ALU.mult).then_inc(s["xn"], 1)

            def dve_batch(dve, i, p, mid, tail, _):
                q = 1 - p
                t = i - 2
                if tail:
                    dve.wait_ge(s["ut"], t + 1)
                    ut = ps_7[:, :].rearrange("q (h r) -> q h r", r=32)
                    nc.vector.reciprocal(rden[:, :], ut[:, :, HD]).then_inc(s["rden"], 1)
                    dve.wait_ge(s["rden"], t + 1)
                    nc.vector.tensor_tensor(an[:, :, :], ut[:, :, 0:HD], rden[:, :].unsqueeze(2).broadcast_to([128, H, HD]),
                                            ALU.mult).then_inc(s["an"], 1)
                if front_on(i):
                    dve.wait_ge(s["q_hi"], i + 1)
                    wait(dve, s["s"], i - 1)
                    nc.vector.scalar_tensor_tensor(q_st[:, p].rearrange("p g q -> p (g q)"), q_hi[:, :, :].rearrange("p g q -> p (g q)"), neg_q,
                                                   ps_6[:, :], ALU.mult, ALU.add).then_inc(s["q_st"], 1)
                    dve.wait_ge(s["k_hi"], i + 1)
                    nc.vector.scalar_tensor_tensor(k_st[:, p].rearrange("p g k -> p (g k)"), k_hi[:, :, :].rearrange("p g k -> p (g k)"), neg_k,
                                                   ps_6[:, 0:G * K2], ALU.mult, ALU.add).then_inc(s["k_st"], 1)
                if tail:
                    dve.wait_ge(s["o"], t + 1)
                    xb = x_all[:, bass.ds(t - o, 1), :].rearrange("s b d -> s (b d)")
                    nc.vector.scalar_tensor_tensor(xb, ps_7[:, 0:128], tg[:, layer:layer + 1], xb, ALU.mult, ALU.add).then_inc(s["x_new"], 1)
                if mid:
                    k = i - 1
                    dve.wait_ge(s["pt0"], k + 1)
                    wait(dve, s["u"], k)
                    nc.vector.tensor_copy(pt_s[:, 0, :, :].rearrange("k g q -> k (g q)"), ps_a[0:K2, :]).then_inc(s["pe0"], 1)
                if front_on(i):
                    dve.wait_ge(s["s"], i + 1)
                    sc = ps_s[:, :, 0:G * K2].rearrange("q j (g k) -> q j g k", g=G)
                    nc.vector.tensor_reduce(mx[:, :].rearrange("q (j g) -> q j g", j=4), sc, AX, ALU.max).then_inc(s["mx"], 1)
                    dve.wait_ge(s["mx"], i + 1)
                    wait(dve, s["p"], i)
                    nc.vector.tensor_tensor(sd[:, :, :, :], sc, mx[:, :].rearrange("q (j g) -> q j g", j=4).unsqueeze(3).broadcast_to([128, 4, G, K2]),
                                            ALU.subtract).then_inc(s["sd"], 1)

            def dve_prog(dve):
                if layer == 0:
                    setup_dve(dve)
                    dve.wait_ge(m["const_ok"], NCONST_OK)
                else:
                    dve.wait_ge(m["phase_end"], 3 * 4)
                norm_stats(dve, o, 0)
                norm_stats(dve, o + 1, 1)
                dve.wait_ge(s["st1"], o + 2)
                norm_aggregate(0)
                norm_aggregate(1)
                normalise(dve, o, 0, 0)
                dve_batch(dve, o, 0, False, False, None)
                norm_stats(dve, o + 2, 0)
                normalise(dve, o + 1, 1, o + 3)
                norm_aggregate(0)
                dve_batch(dve, o + 1, 1, True, False, None)
                norm_stats(dve, o + 3, 1)
                normalise(dve, o + 2, 0, o + 4)
                norm_aggregate(1)
                with dve.Fori(o + 2, o + B - 3, 2) as i:
                    dve_batch(dve, i, 0, True, True, None)
                    norm_stats(dve, i + 2, 0)
                    normalise(dve, i + 1, 1, i + 3)
                    norm_aggregate(0)
                    dve_batch(dve, i + 1, 1, True, True, None)
                    norm_stats(dve, i + 3, 1)
                    normalise(dve, i + 2, 0, i + 4)
                    norm_aggregate(1)
                dve_batch(dve, o + B - 2, 0, True, True, None)
                normalise(dve, o + B - 1, 1, 0)
                dve_batch(dve, o + B - 1, 1, True, True, None)
                dve_batch(dve, o + B, 0, True, True, None)
                dve_batch(dve, o + B + 1, 1, False, True, None)
                phase_end(dve)

            progs["sp"].append(sp_prog)
            progs["pool"].append(pool_prog)
            progs["pe"].append(pe_prog)
            progs["act"].append(act_prog)
            progs["dve"].append(dve_prog)

        def phase_end(eng):
            eng.drain().then_inc(m["phase_end"], 1)

        def router(layer):
            o = layer * NBLK
            n = ("st", "st2", "st3", "st4", "xn", "xt", "hi", "lo", "h", "h_ev", "h_hi", "h_lo", "l", "lg", "lmax", "sub", "exp",
                 "cmp", "cmq", "cms", "cmt", "rank", "sel", "prod", "sum", "rec", "gate")
            s = {k: shared_sem("r_" + k) for k in n}
            base = (1 + 3 * layer) * 4 if layer == 0 else 4 * 4

            def pool_prog(pool):
                pool.wait_ge(m["phase_end"], base)
                with pool.Fori(o, o + NBLK) as i:
                    pool.wait_ge(s["st2"], i + 1)
                    nc.gpsimd.tensor_tensor(rs4[:, :, 0], mv4[:, :, 1], cst[:, C_EPS:C_EPS + TB], ALU.add).then_inc(s["st3"], 1)
                    pool.wait_ge(s["st3"], i + 1)
                    nc.gpsimd.tensor_tensor(rs4[:, :, 0], rs4[:, :, 0], cst[:, C_HALF:C_HALF + TB], ALU.pow).then_inc(s["st4"], 1)
                phase_end(pool)

            def pe_prog(pe):
                pe.wait_ge(m["phase_end"], base)
                with pe.Fori(o, o + NBLK) as i:
                    pe.wait_ge(s["xn"], i + 1)
                    pe.wait_ge(s["lo"], i)
                    for b in range(TB):
                        mm = nc.tensor.transpose(ps_6[:, b * 128:(b + 1) * 128], xn4[:, 0, b, :], ident)
                    mm.then_inc(s["xt"], 1)
                    pe.wait_ge(s["hi"], i + 1)
                    pe.wait_ge(s["lo"], i + 1)
                    if layer == 0:
                        pe.wait_ge(s["lg"], i)
                        for b in range(TB):
                            for k, (a, w) in enumerate(((0, 0), (0, 1), (1, 0))):
                                mm = nc.tensor.matmul(ps_7[:, b * E:(b + 1) * E], xt_hl[:, a, bass.ds((i - o) * TOK + b * 128, 128)],
                                                      rw0_hl[:, w, :], start=k == 0, stop=k == 2)
                        mm.then_inc(s["l"], 1)
                    else:
                        pe.wait_ge(s["h_ev"], i - o)
                        for c in range(C):
                            for k, (a, w) in enumerate(((0, 0), (1, 0), (0, 1))):
                                mm = nc.tensor.matmul(ps_s[:, c, :], rw1_hl[:, w, c * 128:(c + 1) * 128],
                                                      xt_hl[:, a, bass.ds((i - o) * TOK, TOK)], start=k == 0, stop=k == 2)
                        mm.then_inc(s["h"], 1)
                        pe.wait_ge(s["h_lo"], i - o + 1)
                        pe.wait_ge(s["lg"], i)
                        for b in range(TB):
                            o_ = ps_7[:, b * E:(b + 1) * E]
                            nc.tensor.matmul(o_, ones_bf[:, :], bias_bf[:, RB2:RB2 + E], start=True, stop=False)
                            for c in range(C):
                                for k, (a, w) in enumerate(((0, 0), (0, 1), (1, 0))):
                                    mm = nc.tensor.matmul(o_, h_hl[:, 0, a, c, b * 128:(b + 1) * 128], rw2_hl[:, w, c, :],
                                                          start=False, stop=c == C - 1 and k == 2)
                        mm.then_inc(s["l"], 1)
                phase_end(pe)

            def act_prog(act):
                act.wait_ge(m["phase_end"], base)
                with act.Fori(o, o + NBLK) as i:
                    act.wait_ge(s["xt"], i + 1)
                    nc.scalar.activation(xt_hl[:, 0, bass.ds((i - o) * TOK, TOK)], ps_6[:, :], ACT.Copy).then_inc(s["hi"], 1)
                    if layer:
                        act.wait_ge(s["h"], i - o + 1)
                        act.wait_ge(s["h_lo"], i - o)
                        for c in range(C):
                            ins = nc.scalar.activation(h32[:, c, :], ps_s[:, c, :], ACT.Relu, bias=rb1_f[:, c:c + 1])
                        ins.then_inc(s["h_ev"], 1)
                    act.wait_ge(s["sub"], i + 1)
                    nc.scalar.activation(lg[:, :, :], lg[:, :, :], ACT.Exp).then_inc(s["exp"], 1)
                phase_end(act)

            def dve_prog(dve):
                dve.wait_ge(m["phase_end"], base)
                up_tri = cst[:, C_UP:C_UP + 64].rearrange("p (a b) -> p a b", a=E).unsqueeze(1).broadcast_to([128, TB, E, E])
                with dve.Fori(o, o + NBLK) as i:
                    dve.wait_ge(s["xn"], i)
                    for b in range(TB):
                        xb = x_all[:, bass.ds((i - o) * TB + b, 1), :].rearrange("s b d -> s (b d)")
                        ins = nc.vector.bn_stats(st4[:, b, :], xb)
                    ins.then_inc(s["st"], 1)
                    dve.wait_ge(s["st"], i + 1)
                    nc.vector.memset(lmax[:, :], 0.0)
                    for b in range(TB):
                        ins = nc.vector.bn_aggr(mv4[:, b, :], st4[:, b, :])
                    ins.then_inc(s["st2"], 1)
                    dve.wait_ge(s["st4"], i + 1)
                    dve.wait_ge(s["xt"], i)
                    for b in range(TB):
                        xb = x_all[:, bass.ds((i - o) * TB + b, 1), :].rearrange("s b d -> s (b d)")
                        ins = nc.vector.tensor_scalar(xn4[:, 0, b, :], xb, mv4[:, b, 0:1], rs4[:, b, :], ALU.subtract, ALU.mult)
                    ins.then_inc(s["xn"], 1)
                    dve.wait_ge(s["hi"], i + 1)
                    nc.vector.tensor_tensor(xt_hl[:, 1, bass.ds((i - o) * TOK, TOK)], ps_6[:, :], xt_hl[:, 0, bass.ds((i - o) * TOK, TOK)],
                                            ALU.subtract).then_inc(s["lo"], 1)
                    if layer:
                        dve.wait_ge(s["h_ev"], i - o + 1)
                        dve.wait_ge(s["l"], i)
                        nc.vector.tensor_copy(h_hl[:, 0, 0], h32[:, :, :]).then_inc(s["h_hi"], 1)
                        dve.wait_ge(s["h_hi"], i - o + 1)
                        nc.vector.tensor_tensor(h_hl[:, 0, 1], h32[:, :, :], h_hl[:, 0, 0], ALU.subtract).then_inc(s["h_lo"], 1)
                    dve.wait_ge(s["l"], i + 1)
                    dve.wait_ge(s["gate"], i)
                    nc.vector.tensor_copy(lg[:, :, :].rearrange("p b e -> p (b e)"), ps_7[:, 0:TB * E]).then_inc(s["lg"], 1)
                    dve.wait_ge(s["lg"], i + 1)
                    mine = lg[:, :, :].unsqueeze(3).broadcast_to([128, TB, E, E])
                    other = lg[:, :, :].unsqueeze(2).broadcast_to([128, TB, E, E])
                    for b in range(TB):
                        nc.vector.tensor_tensor(cmp_a[:, b], other[:, b], mine[:, b], ALU.is_gt)
                        ins = nc.vector.tensor_tensor(cmp_b[:, b], other[:, b], mine[:, b], ALU.is_equal)
                    ins.then_inc(s["cmp"], 1)
                    nc.vector.tensor_reduce(lmax[:, :], lg[:, :, :], AX, ALU.max).then_inc(s["lmax"], 1)
                    dve.wait_ge(s["cmp"], i + 1)
                    low = cst[:, C_LOW:C_LOW + 64].rearrange("p (a b) -> p a b", a=E)
                    for b in range(TB):
                        ins = nc.vector.tensor_tensor(cmp_b[:, b], cmp_b[:, b], low, ALU.mult)
                    ins.then_inc(s["cmq"], 1)
                    dve.wait_ge(s["cmq"], i + 1)
                    nc.vector.tensor_tensor(cmp_a[:, :, :, :], cmp_a[:, :, :, :], cmp_b[:, :, :, :], ALU.add).then_inc(s["cms"], 1)
                    dve.wait_ge(s["cms"], i + 1)
                    nc.vector.tensor_reduce(rank[:, :, :], cmp_a[:, :, :, :], AX, ALU.add).then_inc(s["rank"], 1)
                    dve.wait_ge(s["lmax"], i + 1)
                    nc.vector.tensor_tensor(lg[:, :, :], lg[:, :, :], lmax[:, :].unsqueeze(2).broadcast_to([128, TB, E]), ALU.subtract).then_inc(s["sub"], 1)
                    dve.wait_ge(s["rank"], i + 1)
                    nc.vector.tensor_scalar(rank[:, :, :], rank[:, :, :], float(TOPK[layer]), None, ALU.is_lt).then_inc(s["sel"], 1)
                    dve.wait_ge(s["sel"], i + 1)
                    dve.wait_ge(s["exp"], i + 1)
                    nc.vector.tensor_tensor(lg[:, :, :], lg[:, :, :], rank[:, :, :], ALU.mult).then_inc(s["prod"], 1)
                    dve.wait_ge(s["prod"], i + 1)
                    nc.vector.tensor_reduce(lsum[:, :], lg[:, :, :], AX, ALU.add).then_inc(s["sum"], 1)
                    dve.wait_ge(s["sum"], i + 1)
                    nc.vector.reciprocal(lsum[:, :], lsum[:, :]).then_inc(s["rec"], 1)
                    dve.wait_ge(s["rec"], i + 1)
                    nc.vector.scalar_tensor_tensor(gate[:, bass.ds((i - o) * TB, TB), :], lg[:, :, :], tg[:, 2 + layer:3 + layer],
                                                   lsum[:, :].unsqueeze(2).broadcast_to([128, TB, E]), ALU.mult, ALU.mult).then_inc(s["gate"], 1)
                phase_end(dve)

            progs["pool"].append(pool_prog)
            progs["pe"].append(pe_prog)
            progs["act"].append(act_prog)
            progs["dve"].append(dve_prog)

        st4 = sb("st4", [128, TB, 6], F32)
        mv4 = sb("mv4", [128, TB, 2], F32)
        rs4 = sb("rs4", [128, TB, 1], F32)

        def experts(layer):
            o = layer * NBLK
            n = ("w_ld", "w_hi", "w_lo", "up", "h_ev", "h_hi", "h_lo", "y", "x_new")
            s = {k: shared_sem("f_" + k) for k in n}
            ups = [shared_sem(f"f_up{c}") for c in range(C)]
            evs = [shared_sem(f"f_ev{c}") for c in range(C)]
            his = [shared_sem(f"f_hi{c}") for c in range(C)]
            los = [shared_sem(f"f_lo{c}") for c in range(C)]
            base = (2 + 3 * layer) * 4

            def sp_prog(sp):
                if layer:
                    sp.wait_ge(m["phase_end"], 3 * 4)
                sp.dma_start(stage[:, :, :], up[layer]).then_inc(s["w_ld"], 16)
                sp.wait_ge(s["w_lo"], 2 * layer + 1)
                sp.dma_start(stage[:, :, :], down[layer]).then_inc(s["w_ld"], 16)

            def split_weights(act, dve):
                for k, dst in enumerate((up_hl[:, :, :, :], down_hl[:, :, :, :, :].rearrange("p t e c d -> p t e (c d)"))):
                    if act is not None:
                        act.wait_ge(s["w_ld"], 16 * (2 * layer + k + 1))
                        nc.scalar.activation(dst[:, 0], stage[:, :, :], ACT.Copy).then_inc(s["w_hi"], 1)
                    else:
                        dve.wait_ge(s["w_hi"], 2 * layer + k + 1)
                        nc.vector.tensor_tensor(dst[:, 1], stage[:, :, :], dst[:, 0], ALU.subtract).then_inc(s["w_lo"], 1)

            def pe_prog(pe):
                pe.wait_ge(m["phase_end"], base)
                pe.wait_ge(s["w_lo"], 2 * layer + 2)

                def up_products(i, e, u):
                    for c in range(C):
                        wait(pe, evs[c], u)
                        for k, (a, w) in enumerate(((0, 0), (1, 0), (0, 1))):
                            mm = nc.tensor.matmul(ps_s[:, c, :], up_hl[:, w, e, c * 128:(c + 1) * 128],
                                                  xt_hl[:, a, bass.ds((i - o) * TOK, TOK)], start=k == 0, stop=k == 2)
                        mm.then_inc(ups[c], 1)

                def down_products(e, u):
                    ps = (ps_a, ps_b)[e % 2]
                    pe.wait_ge(los[C - 1], u + 1)
                    wait(pe, s["x_new"], u - 1)
                    for b in range(TB):
                        o_ = ps[:, b * 128:(b + 1) * 128]
                        if layer:
                            nc.tensor.matmul(o_, ones_bf[:, :], bias_bf[:, B2 + e * D:B2 + (e + 1) * D], start=True, stop=False)
                        for c in range(C):
                            for k, (a, w) in enumerate(((0, 0), (0, 1), (1, 0))):
                                mm = nc.tensor.matmul(o_, h_hl[:, e % 2, a, c, b * 128:(b + 1) * 128], down_hl[:, w, e, c, :],
                                                      start=not layer and c == 0 and k == 0, stop=c == C - 1 and k == 2)
                    mm.then_inc(s["y"], 1)

                up_products(o, 0, o * E)
                for e in range(E):
                    if e < E - 1:
                        up_products(o, e + 1, o * E + e + 1)
                    else:
                        up_products(o + 1, 0, o * E + E)
                    down_products(e, o * E + e)
                with pe.Fori(o + 1, o + NBLK - 1) as i:
                    for e in range(E):
                        if e < E - 1:
                            up_products(i, e + 1, i * E + e + 1)
                        else:
                            up_products(i + 1, 0, i * E + E)
                        down_products(e, i * E + e)
                i = o + NBLK - 1
                for e in range(E):
                    if e < E - 1:
                        up_products(i, e + 1, i * E + e + 1)
                    down_products(e, i * E + e)
                phase_end(pe)

            def act_prog(act):
                act.wait_ge(m["phase_end"], base)
                split_weights(act, None)
                with act.Fori(o, o + NBLK) as i:
                    for e in range(E):
                        u = i * E + e
                        for c in range(C):
                            act.wait_ge(ups[c], u + 1)
                            act.wait_ge(los[c], u)
                            if layer:
                                nc.scalar.activation(h32[:, c, :], ps_s[:, c, :], ACT.Relu, bias=b1_f[:, e, c:c + 1]).then_inc(evs[c], 1)
                            else:
                                nc.scalar.activation(h32[:, c, :], ps_s[:, c, :], ACT.Gelu_apprx_tanh).then_inc(evs[c], 1)
                phase_end(act)

            def pool_prog(pool):
                pool.wait_ge(m["phase_end"], base)
                phase_end(pool)

            def dve_prog(dve):
                dve.wait_ge(m["phase_end"], base)
                split_weights(None, dve)

                def hidden(e, u):
                    for c in range(C):
                        dve.wait_ge(evs[c], u + 1)
                        if c == 0:
                            wait(dve, s["y"], u - 1)
                        nc.vector.tensor_copy(h_hl[:, e % 2, 0, c, :], h32[:, c, :]).then_inc(his[c], 1)
                        dve.wait_ge(his[c], u + 1)
                        nc.vector.tensor_tensor(h_hl[:, e % 2, 1, c, :], h32[:, c, :], h_hl[:, e % 2, 0, c, :], ALU.subtract).then_inc(los[c], 1)

                def residual(i, e, u):
                    ps = (ps_a, ps_b)[e % 2]
                    dve.wait_ge(s["y"], u + 1)
                    wait(dve, s["x_new"], u)
                    for b in range(TB):
                        xb = x_all[:, bass.ds((i - o) * TB + b, 1), :].rearrange("s b d -> s (b d)")
                        gb = gate[:, bass.ds((i - o) * TB + b, 1), e:e + 1].rearrange("s b e -> s (b e)")
                        ins = nc.vector.scalar_tensor_tensor(xb, ps[:, b * 128:(b + 1) * 128], gb, xb, ALU.mult, ALU.add)
                    ins.then_inc(s["x_new"], 1)

                hidden(0, o * E)
                for e in range(E):
                    hidden((e + 1) % 2, o * E + e + 1)
                    residual(o, e, o * E + e)
                with dve.Fori(o + 1, o + NBLK - 1) as i:
                    for e in range(E):
                        hidden((e + 1) % 2, i * E + e + 1)
                        residual(i, e, i * E + e)
                i = o + NBLK - 1
                for e in range(E):
                    if e < E - 1:
                        hidden((e + 1) % 2, i * E + e + 1)
                    residual(i, e, i * E + e)
                phase_end(dve)

            progs["sp"].append(sp_prog)
            progs["pool"].append(pool_prog)
            progs["pe"].append(pe_prog)
            progs["act"].append(act_prog)
            progs["dve"].append(dve_prog)

        for layer in range(2):
            attention(layer)
            router(layer)
            experts(layer)

        def store(sp):
            sp.wait_ge(m["phase_end"], 6 * 4)
            for k in range(8):
                sp.dma_start(out[k * 8:(k + 1) * 8].rearrange("b s d -> s b d"), x_all[:, k * 8:(k + 1) * 8, :]).then_inc(m["out_st"], 16)
            sp.wait_ge(m["out_st"], 128)

        @block.sync
        def _(sp):
            for f in progs["sp"]:
                f(sp)
            store(sp)

        @block.gpsimd
        def _(pool):
            for f in progs["pool"]:
                f(pool)

        @block.scalar
        def _(act):
            for f in progs["act"]:
                f(act)

        @block.vector
        def _(dve):
            for f in progs["dve"]:
                f(dve)

        @block.tensor
        def _(pe):
            for f in progs["pe"]:
                f(pe)


def kernel(**inputs):
    import numpy as np
    import concourse.bacc as bacc
    from concourse import mybir
    from concourse.bass_utils import run_bass_kernel_spmd

    a = {k: np.ascontiguousarray(v) for k, v in inputs.items()}

    def stack(w, rows):
        w = w.reshape((G, 4, 1, HD) + w.shape[1:])
        full = np.zeros((G, 4, 4, HD) + w.shape[4:], w.dtype)
        full[:, :, 0:3] = w
        return full.reshape((G * 128,) + w.shape[4:])

    def stacks(name):
        both = [stack(a[f"L{l}_xattn_{name}"], G).T.reshape(D, G, 128) for l in range(2)]
        return np.ascontiguousarray(np.stack(both, 1))

    def both_t(name):
        return np.ascontiguousarray(np.stack([a[f"L{l}_xattn_{name}"].T for l in range(2)], 1))

    bias = np.concatenate([
        stack(a["L1_xattn_bq"], 0), stack(a["L1_xattn_bk"], 0), a["L1_xattn_bv"], a["L1_xattn_bo"], a["L0_xattn_bo"],
        a["L1_ffn_b2"].reshape(-1), a["L1_ffn_rb2"]])
    row = np.arange(128)
    consts = np.zeros((128, NCONST), np.float32)
    consts[:, C_ID:C_ID + 128] = np.eye(128)
    consts[:, C_NQ] = np.where(row // HD % 4 == 2, -1, 0)
    consts[:, C_NK] = np.where(row // HD % 4 == 1, -1, 0)
    consts[0:3, C_SEL:C_SEL + 3] = np.eye(3)
    consts[:, C_HALF:C_HALF + TB] = -0.5
    consts[:, C_EPS:C_EPS + TB] = EPS
    consts[:, C_UP:C_UP + 64] = np.triu(np.ones((E, E)), 1).reshape(-1)
    consts[:, C_LOW:C_LOW + 64] = np.tril(np.ones((E, E)), -1).reshape(-1)
    small = np.concatenate([
        a["L0_ffn_router_w"], a["L1_ffn_rw1"], a["L1_ffn_rw2"].reshape(C, 128, E).transpose(1, 0, 2).reshape(128, -1),
        a["L1_ffn_b1"].reshape(E, C, 128).transpose(2, 0, 1).reshape(128, -1), a["L1_ffn_rb1"].reshape(C, 128).T], 1)
    up = np.stack([a["L0_ffn_up_w"].transpose(1, 0, 2), a["L1_ffn_W1"].transpose(1, 0, 2)])
    down = np.stack([a[n].reshape(E, C, 128, D).transpose(2, 0, 1, 3).reshape(128, E, C * D) for n in ("L0_ffn_down_w", "L1_ffn_W2")])
    arrays = {
        "x": a["x"], "ctx": a["ctx_1024"], "mask0": a["mask_Bx1xSxS2_if1"], "mask1": a["mask_BxS2_ff1"],
        "gates": np.concatenate([a["g_xattn"], a["g_ffn"]]), "consts": consts,
        "wq": stacks("Wq"), "wk": stacks("Wk"), "wv": both_t("Wv"), "wo": both_t("Wo"),
        "biases": np.ascontiguousarray(np.broadcast_to(bias, (3, NBIAS))), "small": small,
        "up": np.ascontiguousarray(up), "down": np.ascontiguousarray(down),
    }
    nc = bacc.Bacc("TRN2", target_bir_lowering=False, num_devices=1)
    t = {k: nc.dram_tensor(f"in_{k}", v.shape, mybir.dt.from_np(v.dtype), kind="ExternalInput").ap() for k, v in arrays.items()}
    out = nc.dram_tensor("out_0", (B, S, D), mybir.dt.float32, kind="ExternalOutput").ap()
    flamingo(nc, t["x"], t["ctx"], t["mask0"], t["mask1"], t["gates"], t["consts"], t["wq"], t["wk"], t["wv"], t["wo"],
             t["biases"], t["small"], t["up"], t["down"], None, None, None, None, out)
    r = run_bass_kernel_spmd(nc, [{f"in_{k}": np.ascontiguousarray(v) for k, v in arrays.items()}], core_ids=[0])
    return r.results[0]["out_0"]
```

```python
from contextlib import ExitStack

import numpy as np

import concourse.bass as bass
from concourse import mybir

F32 = mybir.dt.float32
F16 = mybir.dt.float16
BF16 = mybir.dt.bfloat16
I32 = mybir.dt.int32
ALU = mybir.AluOpType
ACT = mybir.ActivationFunctionType
AX = mybir.AxisListType.X

B, S, D = 64, 128, 128
K2 = 77
H, HD = 16, 8
G = 4
E, HID = 8, 512
C = HID // 128
TB = 4
NBLK = B // TB
TOK = TB * S
TOPK = (4, 2)
FREE = 320
INV = 1.0 / np.sqrt(np.float32(HD))
PEN0 = float(-1e20 * INV)
FMIN = float(np.finfo(np.float32).min)
EPS = 1e-5

BQ, BK, BV, BO1, BO0, B2, RB2 = 0, 512, 1024, 1152, 1280, 1408, 1408 + E * D
NBIAS = RB2 + E
C_ID, C_NQ, C_NK, C_SEL, C_UP, C_LOW, C_HALF, C_EPS = 0, 128, 129, 130, 133, 197, 261, 265
NCONST = C_EPS + TB


def wait(eng, sem, value):
    if isinstance(value, int) and value <= 0:
        return
    eng.wait_ge(sem, value)


def loaded(i, p):
    return 8 * (i - p) + 16


def flamingo(nc, x, ctx_in, mask0, mask1, gates_in, consts, wq, wk, wv, wo, biases, rw0, up, down, rw1, rw2, b1, rb1, out):
    with ExitStack() as ctx:
        def sb(name, shape, dt):
            return ctx.enter_context(nc.sbuf_tensor(name, shape, dt))

        def sem(name):
            return ctx.enter_context(nc.semaphore(name))

        made = {}

        def shared_sem(name):
            if name not in made:
                made[name] = sem(name)
            return made[name]

        x_all = sb("x_all", [128, B, D], F32)
        cst = sb("cst", [128, NCONST], F32)
        ident_bf = sb("ident_bf", [128, 128], BF16)
        ones_all = sb("ones_all", [128, 128], BF16)
        ones_bf = ones_all[0:3, :]
        tg = sb("tg", [128, 4], F32)
        wq_s = sb("wq_s", [128, 2, G, 128], F32)
        wk_s = sb("wk_s", [128, 2, G, 128], F32)
        wv_s = sb("wv_s", [128, 2, 128], F32)
        wo_s = sb("wo_s", [128, 2, 128], F32)
        bias_bf = sb("bias_bf", [3, NBIAS], BF16)
        pen_f = sb("pen_f", [B, 4, K2], F32)
        pen_parts = sb("pen_parts", [B, 3, K2], BF16)
        pen1 = sb("pen1", [128, B, K2], BF16)
        stage = sb("stage", [128, E, HID], F32)
        up_hl = sb("up_hl", [128, 2, E, HID], F16)
        down_hl = sb("down_hl", [128, 2, E, C, D], F16)
        small_w = sb("small_w", [128, E + HID + C * E + E * C + C], F32)
        rw0_hl = sb("rw0_hl", [128, 2, E], F16)
        rw1_hl = sb("rw1_hl", [128, 2, HID], F16)
        rw2_hl = sb("rw2_hl", [128, 2, C, E], F16)
        ctx_s = sb("ctx_s", [K2, 2, D], F32)
        mask_s = sb("mask_s", [128, 2, K2], I32)
        pen0 = sb("pen0", [128, 2, K2], BF16)
        stats = sb("stats", [128, 2, 6], F32)
        mv = sb("mv", [128, 2, 2], F32)
        rstd = sb("rstd", [128, 2, 1], F32)
        xn = sb("xn", [128, 2, D], F32)
        xc_t = sb("xc_t", [128, 2, 256 + K2], F32)
        q_hi = sb("q_hi", [128, G, 128], F16)
        q_st = sb("q_st", [128, G, 128], F16)
        k_hi = sb("k_hi", [128, G, K2], F16)
        k_st = sb("k_st", [128, G, K2], F16)
        v_s = sb("v_s", [K2, 2, H, 32], F32)
        mx = sb("mx", [128, H], F32)
        sd = sb("sd", [128, 4, G, K2], F32)
        NP, NPT = H * K2, H * 128
        shared = sb("shared", [128, max(NP + NPT, 2 * C * TOK)], F32)
        p_s = shared[:, 0:NP].rearrange("q (j g k) -> q j g k", j=4, g=G)
        pt_s = shared[0:K2, NP:NP + NPT].rearrange("k (j g q) -> k j g q", j=4, g=G)
        u_s = sb("u_s", [128, G, 128], F32)
        rden = sb("rden", [128, H], F32)
        an = sb("an", [128, H, HD], F32)
        xn4 = sb("xn4", [128, TB, D], F32)
        hr_hl = sb("hr_hl", [128, 2, C, 128], F16)
        wide = sb("wide", [128, B * S], F32)
        xt_hl = wide[:, :].bitcast(F16).rearrange("p (a n) -> p a n", a=2)
        bias_f = wide[0:3, 0:3 * NBIAS].rearrange("p (a n) -> p a n", a=3)
        h32 = sb("h32", [128, C, TOK], F32)
        h_hl = shared[:, 0:2 * C * TOK].bitcast(F16).rearrange("p (a t c n) -> p a t c n", a=2, t=2, c=C)
        lg = sb("lg", [128, TB, E], F32)
        cmp_a = sb("cmp_a", [128, TB, E, E], F32)
        cmp_b = sb("cmp_b", [128, TB, E, E], F32)
        rank = sb("rank", [128, TB, E], F32)
        lmax = sb("lmax", [128, TB], F32)
        lsum = sb("lsum", [128, TB], F32)
        gate = sb("gate", [128, B, E], F32)

        ps_s = ctx.enter_context(nc.psum_tensor("ps_s", [128, 4, 512], F32))
        ps_a = ctx.enter_context(nc.psum_tensor("ps_a", [128, 512], F32))
        ps_b = ctx.enter_context(nc.psum_tensor("ps_b", [128, 512], F32))
        ps_6 = ctx.enter_context(nc.psum_tensor("ps_6", [128, 512], F32))
        ps_7 = ctx.enter_context(nc.psum_tensor("ps_7", [128, 512], F32))

        ident = cst[:, C_ID:C_ID + 128]

        names = ("setup_ld", "w_ld", "pen_ld", "const_ok", "bias_ok", "split_ok", "pen_moved", "rsplit_ok",
                 "phase_end", "setup_chain", "out_st")
        m = {n: sem(n) for n in names}
        block = ctx.enter_context(nc.Block())
        progs = {k: [] for k in ("sp", "act", "dve", "pool", "pe")}

        def setup_sp(sp):
            sp.dma_start(cst[:, :], consts).then_inc(m["setup_ld"], 16)
            sp.dma_start(tg[:, :], gates_in.partition_broadcast(128)).then_inc(m["setup_ld"], 16)
            sp.dma_start(wq_s[:, :, :, :], wq).then_inc(m["setup_ld"], 16)
            sp.dma_start(wk_s[:, :, :, :], wk).then_inc(m["setup_ld"], 16)
            sp.dma_start(wv_s[:, :, :], wv).then_inc(m["setup_ld"], 16)
            sp.dma_start(wo_s[:, :, :], wo).then_inc(m["setup_ld"], 16)
            sp.dma_start(bias_f[:, 0, :], biases).then_inc(m["setup_ld"], 16)
            sp.dma_start(pen_f[:, 0, :], mask1).then_inc(m["setup_ld"], 16)
            sp.dma_start(small_w[:, :], rw_all).then_inc(m["setup_ld"], 16)

        NLD = 16 * 9
        rw_all = rw0
        o = 0
        rw0_f = small_w[:, o:o + E]; o += E
        rw1_f = small_w[:, o:o + HID]; o += HID
        rw2_f = small_w[:, o:o + C * E].rearrange("p (c e) -> p c e", c=C); o += C * E
        b1_f = small_w[:, o:o + E * C].rearrange("p (e c) -> p e c", e=E); o += E * C
        rb1_f = small_w[:, o:o + C]

        def setup_pool(pool):
            nc.gpsimd.memset(v_s[:, :, :, :], 0.0).then_inc(m["setup_chain"], 1)
            nc.gpsimd.memset(ones_all[:, :], 0.0).then_inc(m["setup_chain"], 1)
            nc.gpsimd.memset(pen1[:, :, :], 0.0).then_inc(m["const_ok"], 1)
            pool.wait_ge(m["setup_chain"], 2)
            nc.gpsimd.memset(ones_bf[:, :], 1.0).then_inc(m["const_ok"], 1)
            nc.gpsimd.memset(v_s[:, :, :, HD:HD + 1], 1.0).then_inc(m["const_ok"], 1)
            pool.wait_ge(m["setup_ld"], NLD)
            nc.gpsimd.tensor_copy(ident_bf[:, :], ident).then_inc(m["const_ok"], 1)

        def setup_act(act):
            act.wait_ge(m["setup_ld"], NLD)
            nc.scalar.activation(tg[:, :], tg[:, :], ACT.Tanh).then_inc(m["const_ok"], 1)

        def parts(dve, v, chain):
            mask = -65536
            for k in range(1, 3):
                chain(nc.vector.tensor_single_scalar(v[:, k].bitcast(I32), v[:, 0].bitcast(I32), mask, op=ALU.bitwise_and))
                chain(nc.vector.tensor_tensor(v[:, 0], v[:, 0], v[:, k], ALU.subtract))
            chain(nc.vector.tensor_copy(v[:, 3], v[:, 0]))

        def setup_dve(dve):
            count = [0]
            chain_sem = m["bias_ok"]

            def chain(ins):
                count[0] += 1
                ins.then_inc(chain_sem, 1)
                dve.wait_ge(chain_sem, count[0])

            dve.wait_ge(m["setup_ld"], NLD)
            nc.vector.tensor_scalar(wq_s[:, :, :, :], wq_s[:, :, :, :], float(INV), None, ALU.mult).then_inc(m["const_ok"], 1)
            v, part, kept = bias_f[:, 0], bias_f[:, 1], bias_f[:, 2]
            sel = cst[0:3, C_SEL:C_SEL + 3]
            chain(nc.vector.tensor_scalar(v[:, BQ:BQ + 512], v[:, BQ:BQ + 512], float(INV), None, ALU.mult))
            chain(nc.vector.tensor_single_scalar(part.bitcast(I32), v.bitcast(I32), -65536, op=ALU.bitwise_and))
            chain(nc.vector.tensor_tensor(v, v, part, ALU.subtract))
            chain(nc.vector.tensor_scalar(kept, part, sel[:, 0:1], None, ALU.mult))
            chain(nc.vector.tensor_single_scalar(part.bitcast(I32), v.bitcast(I32), -65536, op=ALU.bitwise_and))
            chain(nc.vector.tensor_tensor(v, v, part, ALU.subtract))
            chain(nc.vector.scalar_tensor_tensor(kept, part, sel[:, 1:2], kept, ALU.mult, ALU.add))
            chain(nc.vector.scalar_tensor_tensor(bias_bf[:, :], v, sel[:, 2:3], kept, ALU.mult, ALU.add))
            chain(nc.vector.tensor_scalar(pen_f[:, 0, :], pen_f[:, 0, :], -1.0, 1.0, ALU.mult, ALU.add))
            chain(nc.vector.tensor_scalar(pen_f[:, 0, :], pen_f[:, 0, :], FMIN, None, ALU.mult))
            parts(dve, pen_f, chain)
            chain(nc.vector.tensor_copy(pen_parts[:, :, :], pen_f[:, 1:4, :]))
            for k, (hl, w) in enumerate(((rw0_hl, rw0_f), (rw1_hl, rw1_f), (rw2_hl, rw2_f))):
                chain(nc.vector.tensor_copy(hl[:, 0], w))
                chain(nc.vector.tensor_tensor(hl[:, 1], w, hl[:, 0], ALU.subtract))
            assert count[0] == BIAS_STEPS

        BIAS_STEPS = 8 + 2 + 5 + 1 + 6
        NCONST_OK = 6

        def pen_sp(sp):
            sp.wait_ge(m["bias_ok"], BIAS_STEPS)
            sp.wait_ge(m["const_ok"], NCONST_OK)
            for k in range(3):
                sp.dma_start(pen1[k:k + 1, :, :], pen_parts[:, k, :]).then_inc(m["pen_moved"], 16)

        def attention(layer):
            o = layer * B
            n = ("x_ld0", "x_ld1", "ctx_ld0", "ctx_ld1", "mask_ld0", "mask_ld1", "pen", "st1", "st2", "st3", "st4", "xn", "xct", "xct_ev", "q", "q_hi", "q_st",
                 "kv", "v_ev", "k_hi", "k_st", "s", "mx", "sd", "p", "pt0", "pt1", "pt2", "pt3", "pe0", "pe1", "pe2", "pe3",
                 "u", "u_ev", "ut", "rden", "an", "o", "x_new")
            s = {k: shared_sem("a_" + k) for k in n}
            neg_q, neg_k = cst[:, C_NQ:C_NQ + 1], cst[:, C_NK:C_NK + 1]

            CHAIN = 3 if layer else 1
            rn = ("st", "st2", "st3", "st4", "xn", "xt", "hi", "lo", "hid", "h_ev", "h_hi", "h_lo", "l", "lg", "lmax", "sub", "exp",
                  "cmp", "cmq", "cms", "rank", "sel", "prod", "sum", "rec", "gate")
            z = {k: shared_sem("r_" + k) for k in rn}
            OR = layer * NBLK

            def xct_of(i):
                return i + 1 + 3 * layer

            def on(i):
                return not isinstance(i, int) or o <= i < o + B

            def block_on(r):
                return not isinstance(r, int) or OR <= r < OR + NBLK

            def steps(eng, f):
                for r in (0, 1):
                    for b in range(TB):
                        f(eng, OR + r, b)
                with eng.Fori(OR + 2, OR + NBLK - 1) as r:
                    for b in range(TB):
                        f(eng, r, b)
                for r in (NBLK - 1, NBLK, NBLK + 1):
                    for b in range(TB):
                        f(eng, OR + r, b)

            def load(sp, i, p):
                if layer == 0:
                    wait(sp, s["st1"], i - 1)
                    sp.dma_start(x_all[:, bass.ds(i - o, 1), :], x[bass.ds(i - o, 1), :, :].rearrange("b s d -> s b d")).then_inc(s[f"x_ld{p}"], 16)
                wait(sp, s["xct"], xct_of(i - 2))
                sp.dma_start(ctx_s[:, p, :], ctx_in[bass.ds(i - o, 1), :, :].rearrange("b s d -> s (b d)")).then_inc(s[f"ctx_ld{p}"], 16)
                if layer == 0:
                    wait(sp, s["pen"], i - 1)
                    sp.dma_start(mask_s[:, p, :], mask0[bass.ds(i - o, 1), 0, :, :].rearrange("b s k -> s (b k)")).then_inc(s[f"mask_ld{p}"], 16)

            def sp_prog(sp):
                if layer == 0:
                    setup_sp(sp)
                else:
                    sp.wait_ge(m["phase_end"], 2 * 4)
                load(sp, o, 0)
                load(sp, o + 1, 1)
                if layer == 0:
                    pen_sp(sp)
                with sp.Fori(o + 2, o + B - 1, 2) as i:
                    load(sp, i, 0)
                    load(sp, i + 1, 1)

            def pool_batch(pool, i, p):
                if layer == 0:
                    wait(pool, s[f"mask_ld{p}"], loaded(i, p))
                    wait(pool, s["s"], i - 1)
                wait(pool, s["st2"], i + 1)
                nc.gpsimd.tensor_tensor(rstd[:, p, :], mv[:, p, 1:2], cst[:, C_EPS:C_EPS + 1], ALU.add).then_inc(s["st3"], 1)
                if layer == 0:
                    nc.gpsimd.tensor_scalar(pen0[:, p, :], mask_s[:, p, :], 0, PEN0, ALU.is_equal, ALU.mult).then_inc(s["pen"], 1)
                wait(pool, s["st3"], i + 1)
                nc.gpsimd.tensor_tensor(rstd[:, p, :], rstd[:, p, :], cst[:, C_HALF:C_HALF + 1], ALU.pow).then_inc(s["st4"], 1)

            def pool_step(pool, r, b):
                i = r * TB + b
                if b == 2 and block_on(r - 1):
                    R = r - 1
                    pool.wait_ge(z["st2"], R + 1)
                    nc.gpsimd.tensor_tensor(rs4[:, :, 0], mv4[:, :, 1], cst[:, C_EPS:C_EPS + TB], ALU.add).then_inc(z["st3"], 1)
                    pool.wait_ge(z["st3"], R + 1)
                    nc.gpsimd.tensor_tensor(rs4[:, :, 0], rs4[:, :, 0], cst[:, C_HALF:C_HALF + TB], ALU.pow).then_inc(z["st4"], 1)
                if on(i + 2):
                    pool_batch(pool, i + 2, b % 2)

            def pool_prog(pool):
                if layer == 0:
                    setup_pool(pool)
                pool_batch(pool, o, 0)
                pool_batch(pool, o + 1, 1)
                steps(pool, pool_step)
                phase_end(pool)

            def next_transposes(pe, i, p):
                pe.wait_ge(s["xn"], i + 1)
                pe.wait_ge(s[f"ctx_ld{p}"], loaded(i, p))
                nc.tensor.transpose(ps_7[:, 128:256], xn[:, p, :], ident)
                return nc.tensor.transpose(ps_7[:, 256:256 + K2], ctx_s[:, p, :], ident[0:K2, 0:K2])

            def prob_transposes(j, sem_):
                ps = (ps_a, ps_b)[j % 2]
                for g in range(G):
                    mm = nc.tensor.transpose(ps[0:K2, g * 128:(g + 1) * 128], p_s[:, j, g, :], ident)
                mm.then_inc(sem_, 1)

            def token_transposes(pe, R):
                pe.wait_ge(z["xn"], R + 1)
                if layer:
                    wait(pe, z["h_ev"], R * TB - o)
                for b in range(TB):
                    mm = nc.tensor.transpose(ps_s[:, b, FREE:FREE + 128], xn4[:, b, :], ident)
                mm.then_inc(z["xt"], 1)

            def router_hidden(pe, R, b):
                if b == 0:
                    pe.wait_ge(z["hi"], R + 1)
                    pe.wait_ge(z["lo"], R + 1)
                else:
                    pe.wait_ge(z["h_ev"], R * TB - o + b)
                for c in range(C):
                    for k, (a, w) in enumerate(((0, 0), (1, 0), (0, 1))):
                        mm = nc.tensor.matmul(ps_s[:, c, FREE:FREE + 128], rw1_hl[:, w, c * 128:(c + 1) * 128],
                                              xt_hl[:, a, bass.ds((R - OR) * TOK + b * 128, 128)], start=k == 0, stop=k == 2)
                mm.then_inc(z["hid"], 1)

            def router_logits(pe, R, b):
                o_ = ps_s[:, 0, FREE + 128 + b * E:FREE + 128 + (b + 1) * E]
                if layer == 0:
                    for k, (a, w) in enumerate(((0, 0), (0, 1), (1, 0))):
                        mm = nc.tensor.matmul(o_, xt_hl[:, a, bass.ds((R - OR) * TOK + b * 128, 128)], rw0_hl[:, w, :],
                                              start=k == 0, stop=k == 2)
                else:
                    pe.wait_ge(z["h_lo"], R * TB - o + b + 1)
                    nc.tensor.matmul(o_, ones_bf[:, :], bias_bf[:, RB2:RB2 + E], start=True, stop=False)
                    for c in range(C):
                        for k, (a, w) in enumerate(((0, 0), (0, 1), (1, 0))):
                            mm = nc.tensor.matmul(o_, hr_hl[:, a, c, :], rw2_hl[:, w, c, :], start=False, stop=c == C - 1 and k == 2)
                mm.then_inc(z["l"], 1)

            def pe_step(pe, r, b):
                i = r * TB + b
                p = b % 2
                q = 1 - p
                k, t = i - 1, i - 2
                mid, tail = on(k), on(t)
                if on(i):
                    pe.wait_ge(s["xct_ev"], xct_of(i))
                    wait(pe, s["k_st"], i)
                    for g in range(G):
                        o_ = ps_6[:, g * 128:(g + 1) * 128]
                        mm = nc.tensor.matmul(o_, wq_s[:, layer, g, :], xc_t[:, p, 128:256], start=True, stop=layer == 0)
                        if layer:
                            mm = nc.tensor.matmul(o_, bias_bf[:, BQ + g * 128:BQ + (g + 1) * 128], ones_bf[:, :], start=False, stop=True)
                    mm.then_inc(s["q"], 1)
                if tail:
                    pe.wait_ge(s["pe2"], t + 1)
                    pe.wait_ge(s["pe3"], t + 1)
                    for g in range(G):
                        for j in range(4):
                            mm = nc.tensor.matmul(ps_a[32 * j:32 * j + 32, g * 128:(g + 1) * 128], v_s[:, p, 4 * g + j, :],
                                                  pt_s[:, j, g, :], start=True, stop=True)
                    mm.then_inc(s["u"], 1)
                if b == 3 and block_on(r - 1):
                    wait(pe, s["sd"], min(i, o + B) if isinstance(i, int) else i)
                    token_transposes(pe, r - 1)
                if layer and b < 3 and block_on(r - 2):
                    wait(pe, s["sd"], min(i, o + B) if isinstance(i, int) else i)
                    router_hidden(pe, r - 2, b + 1)
                if on(i):
                    pe.wait_ge(s["q_st"], i + 1)
                    for g in range(G):
                        o_ = ps_6[:, g * K2:(g + 1) * K2]
                        nc.tensor.matmul(o_, wk_s[:, layer, g, :], xc_t[:, p, 256:256 + K2], start=True, stop=layer == 0)
                        if layer:
                            nc.tensor.matmul(o_, bias_bf[:, BK + g * 128:BK + (g + 1) * 128], ones_bf[:, 0:K2], start=False, stop=True)
                    o_ = ps_6[0:K2, G * K2:G * K2 + 128]
                    mm = nc.tensor.matmul(o_, xc_t[:, p, 256:256 + K2], wv_s[:, layer, :], start=True, stop=layer == 0)
                    if layer:
                        mm = nc.tensor.matmul(o_, ones_bf[:, 0:K2], bias_bf[:, BV:BV + 128], start=False, stop=True)
                    mm.then_inc(s["kv"], 1)
                if tail:
                    pe.wait_ge(s["u_ev"], t + 1)
                    wait(pe, s["x_new"], t)
                    for g in range(G):
                        mm = nc.tensor.transpose(ps_7[:, g * 128:(g + 1) * 128], u_s[:, g, :], ident)
                    mm.then_inc(s["ut"], 1)
                if mid:
                    pe.wait_ge(s["p"], k + 1)
                    prob_transposes(0, s["pt0"])
                    wait(pe, s["pe3"], k)
                    prob_transposes(1, s["pt1"])
                if layer and block_on(r - 2):
                    if b < 3:
                        pe.wait_ge(z["h_ev"], (r - 2) * TB - o + b + 2)
                    elif block_on(r - 1):
                        pe.wait_ge(z["lo"], r)
                    router_logits(pe, r - 2, b)
                if layer and b == 3 and block_on(r - 1):
                    if block_on(r - 2):
                        pe.wait_ge(z["lg"], r - 1)
                    router_hidden(pe, r - 1, 0)
                if not layer and b == 0 and block_on(r - 2):
                    pe.wait_ge(z["hi"], r - 1)
                    pe.wait_ge(z["lo"], r - 1)
                    for b_ in range(TB):
                        router_logits(pe, r - 2, b_)
                if tail:
                    pe.wait_ge(s["an"], t + 1)
                    mm = nc.tensor.transpose(ps_7[:, 0:128], an[:, :, :].rearrange("q h d -> q (h d)"), ident)
                if on(i + 1):
                    if not tail:
                        pe.wait_ge(s["xct_ev"], xct_of(i))
                    mm = next_transposes(pe, i + 1, q)
                if tail or on(i + 1):
                    mm.then_inc(s["xct"], 1)
                if on(i):
                    pe.wait_ge(s["k_st"], i + 1)
                    if layer == 0:
                        pe.wait_ge(s["pen"], i + 1)
                    wait(pe, s["sd"], i)
                    if b == CHAIN and block_on(r - 2):
                        pe.wait_ge(z["lg"], r - 1)
                    if b == 3 and block_on(r - 1):
                        if layer:
                            pe.wait_ge(z["h_ev"], (r - 1) * TB - o + 1)
                        else:
                            pe.wait_ge(z["lo"], r)
                    for j in range(4):
                        o_ = ps_s[:, j, 0:G * K2].rearrange("q (g k) -> q g k", g=G)
                        if layer == 0:
                            nc.tensor.matmul(o_, ident_bf[:, :], pen0[:, p:p + 1, :].broadcast_to([128, G, K2]), start=True, stop=True)
                        else:
                            nc.tensor.matmul(o_, ones_all[:, :], pen1[:, bass.ds(i - o, 1), :].broadcast_to([128, G, K2]), start=True, stop=True)
                    for g in range(G):
                        for j in range(4):
                            r = 32 * j
                            mm = nc.tensor.matmul(ps_s[:, j, g * K2:(g + 1) * K2], q_st[r:r + 32, g, :], k_st[r:r + 32, g, :],
                                                  start=False, stop=True, skip_group_check=True)
                    mm.then_inc(s["s"], 1)
                if tail:
                    pe.wait_ge(s["xct_ev"], xct_of(i + 1))
                    nc.tensor.matmul(ps_7[:, 0:128], xc_t[:, q, 0:128], wo_s[:, layer, :], start=True, stop=False)
                    bo = BO1 if layer else BO0
                    nc.tensor.matmul(ps_7[:, 0:128], ones_bf[:, :], bias_bf[:, bo:bo + 128], start=False, stop=True).then_inc(s["o"], 1)
                if mid:
                    for j in (2, 3):
                        pe.wait_ge(s[f"pe{j - 2}"], k + 1)
                        prob_transposes(j, s[f"pt{j}"])

            def pe_prog(pe):
                if layer == 0:
                    pe.wait_ge(m["setup_ld"], NLD)
                    pe.wait_ge(m["const_ok"], NCONST_OK)
                    pe.wait_ge(m["bias_ok"], BIAS_STEPS)
                else:
                    pe.wait_ge(m["pen_moved"], 48)
                    pe.wait_ge(m["phase_end"], 2 * 4)
                next_transposes(pe, o, 0).then_inc(s["xct"], 1)
                steps(pe, pe_step)
                phase_end(pe)

            def evacuate_transposes(act, i, p, first, last):
                act.wait_ge(s["xct"], xct_of(i))
                nc.scalar.activation(xc_t[:, p, first:last], ps_7[:, first:last], ACT.Copy).then_inc(s["xct_ev"], 1)

            def router_relu(act, R, b):
                act.wait_ge(z["hid"], R * TB - o + b + 1)
                wait(act, z["h_lo"], R * TB - o + b)
                for c in range(C):
                    ins = nc.scalar.activation(h32[:, c, 0:128], ps_s[:, c, FREE:FREE + 128], ACT.Relu, bias=rb1_f[:, c:c + 1])
                ins.then_inc(z["h_ev"], 1)

            def act_step(act, r, b):
                i = r * TB + b
                p = b % 2
                q = 1 - p
                k, t = i - 1, i - 2
                mid, tail = on(k), on(t)
                if on(i):
                    act.wait_ge(s["q"], i + 1)
                    wait(act, s["q_st"], i)
                    nc.scalar.activation(q_hi[:, :, :].rearrange("p g q -> p (g q)"), ps_6[:, :], ACT.Copy).then_inc(s["q_hi"], 1)
                if tail:
                    act.wait_ge(s["u"], t + 1)
                    nc.scalar.activation(u_s[:, :, :].rearrange("p g q -> p (g q)"), ps_a[:, :], ACT.Copy).then_inc(s["u_ev"], 1)
                if b == 3 and block_on(r - 1):
                    act.wait_ge(z["xt"], r)
                    nc.scalar.activation(xt_hl[:, 0, bass.ds((r - 1 - OR) * TOK, TOK)].rearrange("d (b s) -> d b s", b=TB),
                                         ps_s[:, :, FREE:FREE + 128], ACT.Copy).then_inc(z["hi"], 1)
                if mid:
                    act.wait_ge(s["sd"], k + 1)
                    wait(act, s["pt3"], k)
                    nc.scalar.activation(p_s[:, :, :, :].rearrange("q j g k -> q (j g k)"), sd[:, :, :, :].rearrange("q j g k -> q (j g k)"),
                                         ACT.Exp).then_inc(s["p"], 1)
                if on(i):
                    act.wait_ge(s["kv"], i + 1)
                    nc.scalar.activation(v_s[:, p, :, 0:HD], ps_6[0:K2, G * K2:G * K2 + 128].rearrange("k (h d) -> k h d", h=H),
                                         ACT.Copy).then_inc(s["v_ev"], 1)
                    wait(act, s["k_st"], i)
                    nc.scalar.activation(k_hi[:, :, :].rearrange("p g k -> p (g k)"), ps_6[:, 0:G * K2], ACT.Copy).then_inc(s["k_hi"], 1)
                if layer and b < 3 and block_on(r - 2):
                    router_relu(act, r - 2, b + 1)

                def evacuate(j):
                    act.wait_ge(s[f"pt{j}"], k + 1)
                    ps = (ps_a, ps_b)[j % 2]
                    nc.scalar.activation(pt_s[:, j, :, :].rearrange("k g q -> k (g q)"), ps[0:K2, :], ACT.Copy).then_inc(s[f"pe{j}"], 1)

                if mid:
                    evacuate(0)
                    evacuate(1)
                if tail or on(i + 1):
                    evacuate_transposes(act, i + 1, q, 0 if tail else 128, 256 + K2 if on(i + 1) else 128)
                if layer and b == 3 and block_on(r - 1):
                    router_relu(act, r - 1, 0)
                if mid:
                    evacuate(2)
                if b == CHAIN and block_on(r - 2):
                    act.wait_ge(z["sub"], r - 1)
                    nc.scalar.activation(lg[:, :, :], lg[:, :, :], ACT.Exp).then_inc(z["exp"], 1)
                if mid:
                    evacuate(3)

            def act_prog(act):
                if layer == 0:
                    setup_act(act)
                    act.wait_ge(m["const_ok"], NCONST_OK)
                else:
                    act.wait_ge(m["phase_end"], 2 * 4)
                evacuate_transposes(act, o, 0, 128, 256 + K2)
                steps(act, act_step)
                phase_end(act)

            def norm_stats(dve, i, p):
                xb = x_all[:, bass.ds(i - o, 1), :].rearrange("s b d -> s (b d)")
                if layer == 0:
                    wait(dve, s[f"x_ld{p}"], loaded(i, p))
                wait(dve, s["xn"], i - 1)
                nc.vector.bn_stats(stats[:, p, :], xb).then_inc(s["st1"], 1)

            def norm_aggregate(p):
                nc.vector.bn_aggr(mv[:, p, :], stats[:, p, :]).then_inc(s["st2"], 1)

            def normalise(dve, i, p, n):
                wait(dve, s["st1"], n)
                wait(dve, s["st4"], i + 1)
                wait(dve, s["xct"], xct_of(i - 2))
                nc.vector.tensor_scalar(xn[:, p, :], x_all[:, bass.ds(i - o, 1), :].rearrange("s b d -> s (b d)"), mv[:, p, 0:1], rstd[:, p, :],
                                        ALU.subtract, ALU.mult).then_inc(s["xn"], 1)

            def router_pick(dve, R):
                dve.wait_ge(z["l"], R * TB + TB)
                nc.vector.tensor_copy(lg[:, :, :].rearrange("p b e -> p (b e)"), ps_s[:, 0, FREE + 128:FREE + 128 + TB * E]).then_inc(z["lg"], 1)
                dve.wait_ge(z["lg"], R + 1)
                mine = lg[:, :, :].unsqueeze(3).broadcast_to([128, TB, E, E])
                other = lg[:, :, :].unsqueeze(2).broadcast_to([128, TB, E, E])
                for b in range(TB):
                    nc.vector.tensor_tensor(cmp_a[:, b], other[:, b], mine[:, b], ALU.is_gt)
                    ins = nc.vector.tensor_tensor(cmp_b[:, b], other[:, b], mine[:, b], ALU.is_equal)
                ins.then_inc(z["cmp"], 1)
                nc.vector.tensor_reduce(lmax[:, :], lg[:, :, :], AX, ALU.max).then_inc(z["lmax"], 1)
                dve.wait_ge(z["lmax"], R + 1)
                nc.vector.tensor_tensor(lg[:, :, :], lg[:, :, :], lmax[:, :].unsqueeze(2).broadcast_to([128, TB, E]), ALU.subtract).then_inc(z["sub"], 1)
                dve.wait_ge(z["cmp"], R + 1)
                low = cst[:, C_LOW:C_LOW + 64].rearrange("p (a b) -> p a b", a=E)
                for b in range(TB):
                    ins = nc.vector.tensor_tensor(cmp_b[:, b], cmp_b[:, b], low, ALU.mult)
                ins.then_inc(z["cmq"], 1)
                dve.wait_ge(z["cmq"], R + 1)
                nc.vector.tensor_tensor(cmp_a[:, :, :, :], cmp_a[:, :, :, :], cmp_b[:, :, :, :], ALU.add).then_inc(z["cms"], 1)
                dve.wait_ge(z["cms"], R + 1)
                nc.vector.tensor_reduce(rank[:, :, :], cmp_a[:, :, :, :], AX, ALU.add).then_inc(z["rank"], 1)
                dve.wait_ge(z["rank"], R + 1)
                nc.vector.tensor_scalar(rank[:, :, :], rank[:, :, :], float(TOPK[layer]), None, ALU.is_lt).then_inc(z["sel"], 1)

            def router_gates(dve, R):
                dve.wait_ge(z["sel"], R + 1)
                dve.wait_ge(z["exp"], R + 1)
                nc.vector.tensor_tensor(lg[:, :, :], lg[:, :, :], rank[:, :, :], ALU.mult).then_inc(z["prod"], 1)
                dve.wait_ge(z["prod"], R + 1)
                nc.vector.tensor_reduce(lsum[:, :], lg[:, :, :], AX, ALU.add).then_inc(z["sum"], 1)
                dve.wait_ge(z["sum"], R + 1)
                nc.vector.reciprocal(lsum[:, :], lsum[:, :]).then_inc(z["rec"], 1)
                dve.wait_ge(z["rec"], R + 1)
                nc.vector.scalar_tensor_tensor(gate[:, bass.ds((R - OR) * TB, TB), :], lg[:, :, :], tg[:, 2 + layer:3 + layer],
                                               lsum[:, :].unsqueeze(2).broadcast_to([128, TB, E]), ALU.mult, ALU.mult).then_inc(z["gate"], 1)

            def router_split(dve, R, b):
                dve.wait_ge(z["h_ev"], R * TB - o + b + 1)
                wait(dve, z["l"], R * TB + b)
                nc.vector.tensor_copy(hr_hl[:, 0], h32[:, :, 0:128]).then_inc(z["h_hi"], 1)
                dve.wait_ge(z["h_hi"], R * TB - o + b + 1)
                nc.vector.tensor_tensor(hr_hl[:, 1], h32[:, :, 0:128], hr_hl[:, 0], ALU.subtract).then_inc(z["h_lo"], 1)

            def token_rows(R, b):
                return x_all[:, bass.ds((R - OR) * TB + b, 1), :].rearrange("s b d -> s (b d)")

            def dve_step(dve, r, b):
                i = r * TB + b
                p = b % 2
                q = 1 - p
                t = i - 2
                tail = on(t)
                if on(i):
                    dve.wait_ge(s["q_hi"], i + 1)
                    nc.vector.scalar_tensor_tensor(q_st[:, :, :].rearrange("p g q -> p (g q)"), q_hi[:, :, :].rearrange("p g q -> p (g q)"), neg_q,
                                                   ps_6[:, :], ALU.mult, ALU.add).then_inc(s["q_st"], 1)
                if b == 2 and block_on(r - 1):
                    dve.wait_ge(s["x_new"], t)
                    for b_ in range(TB):
                        ins = nc.vector.bn_stats(st4[:, b_, :], token_rows(r - 1, b_))
                    ins.then_inc(z["st"], 1)
                if on(i + 2):
                    norm_stats(dve, i + 2, p)
                if on(i + 1):
                    normalise(dve, i + 1, q, i + 3 if on(i + 2) else 0)
                if on(i + 2):
                    norm_aggregate(p)
                if layer and block_on(r - 2):
                    router_split(dve, r - 2, b)
                if on(i):
                    dve.wait_ge(s["k_hi"], i + 1)
                    nc.vector.scalar_tensor_tensor(k_st[:, :, :].rearrange("p g k -> p (g k)"), k_hi[:, :, :].rearrange("p g k -> p (g k)"), neg_k,
                                                   ps_6[:, 0:G * K2], ALU.mult, ALU.add).then_inc(s["k_st"], 1)
                if b == 2 and block_on(r - 1):
                    dve.wait_ge(z["st"], r)
                    nc.vector.memset(lmax[:, :], 0.0)
                    for b_ in range(TB):
                        ins = nc.vector.bn_aggr(mv4[:, b_, :], st4[:, b_, :])
                    ins.then_inc(z["st2"], 1)
                if b == 3 and block_on(r - 1):
                    dve.wait_ge(z["hi"], r)
                    xt = xt_hl[:, :, bass.ds((r - 1 - OR) * TOK, TOK)].rearrange("d a (b s) -> d a b s", b=TB)
                    nc.vector.tensor_tensor(xt[:, 1], ps_s[:, :, FREE:FREE + 128], xt[:, 0], ALU.subtract).then_inc(z["lo"], 1)
                if tail:
                    dve.wait_ge(s["ut"], t + 1)
                    ut = ps_7[:, :].rearrange("q (h r) -> q h r", r=32)
                    nc.vector.reciprocal(rden[:, :], ut[:, :, HD]).then_inc(s["rden"], 1)
                    dve.wait_ge(s["rden"], t + 1)
                    nc.vector.tensor_tensor(an[:, :, :], ut[:, :, 0:HD], rden[:, :].unsqueeze(2).broadcast_to([128, H, HD]),
                                            ALU.mult).then_inc(s["an"], 1)
                if b == CHAIN and block_on(r - 2):
                    router_pick(dve, r - 2)
                sc = ps_s[:, :, 0:G * K2].rearrange("q j (g k) -> q j g k", g=G)
                if on(i):
                    dve.wait_ge(s["s"], i + 1)
                    nc.vector.tensor_reduce(mx[:, :].rearrange("q (j g) -> q j g", j=4), sc, AX, ALU.max).then_inc(s["mx"], 1)
                if tail:
                    dve.wait_ge(s["o"], t + 1)
                    xb = x_all[:, bass.ds(t - o, 1), :].rearrange("s b d -> s (b d)")
                    nc.vector.scalar_tensor_tensor(xb, ps_7[:, 0:128], tg[:, layer:layer + 1], xb, ALU.mult, ALU.add).then_inc(s["x_new"], 1)
                if b == 2 and block_on(r - 1):
                    dve.wait_ge(z["st4"], r)
                    for b_ in range(TB):
                        ins = nc.vector.tensor_scalar(xn4[:, b_, :], token_rows(r - 1, b_), mv4[:, b_, 0:1], rs4[:, b_, :], ALU.subtract, ALU.mult)
                    ins.then_inc(z["xn"], 1)
                if on(i):
                    dve.wait_ge(s["mx"], i + 1)
                    wait(dve, s["p"], i)
                    nc.vector.tensor_tensor(sd[:, :, :, :], sc, mx[:, :].rearrange("q (j g) -> q j g", j=4).unsqueeze(3).broadcast_to([128, 4, G, K2]),
                                            ALU.subtract).then_inc(s["sd"], 1)
                if b == CHAIN and block_on(r - 2):
                    router_gates(dve, r - 2)

            def dve_prog(dve):
                if layer == 0:
                    setup_dve(dve)
                    dve.wait_ge(m["const_ok"], NCONST_OK)
                else:
                    dve.wait_ge(m["phase_end"], 2 * 4)
                norm_stats(dve, o, 0)
                norm_stats(dve, o + 1, 1)
                dve.wait_ge(s["st1"], o + 2)
                norm_aggregate(0)
                norm_aggregate(1)
                normalise(dve, o, 0, 0)
                steps(dve, dve_step)
                phase_end(dve)

            progs["sp"].append(sp_prog)
            progs["pool"].append(pool_prog)
            progs["pe"].append(pe_prog)
            progs["act"].append(act_prog)
            progs["dve"].append(dve_prog)

        def phase_end(eng):
            eng.drain().then_inc(m["phase_end"], 1)

        st4 = sb("st4", [128, TB, 6], F32)
        mv4 = sb("mv4", [128, TB, 2], F32)
        rs4 = sb("rs4", [128, TB, 1], F32)

        def experts(layer):
            o = layer * NBLK
            n = ("w_ld", "w_hi", "w_lo", "up", "h_ev", "h_hi", "h_lo", "y", "x_new")
            s = {k: shared_sem("f_" + k) for k in n}
            ups = [shared_sem(f"f_up{c}") for c in range(C)]
            evs = [shared_sem(f"f_ev{c}") for c in range(C)]
            his = [shared_sem(f"f_hi{c}") for c in range(C)]
            los = [shared_sem(f"f_lo{c}") for c in range(C)]
            base = (1 + 2 * layer) * 4

            def sp_prog(sp):
                if layer:
                    sp.wait_ge(m["phase_end"], 2 * 4)
                sp.dma_start(stage[:, :, :], up[layer]).then_inc(s["w_ld"], 16)
                sp.wait_ge(s["w_lo"], 2 * layer + 1)
                sp.dma_start(stage[:, :, :], down[layer]).then_inc(s["w_ld"], 16)

            def split_weights(act, dve):
                for k, dst in enumerate((up_hl[:, :, :, :], down_hl[:, :, :, :, :].rearrange("p t e c d -> p t e (c d)"))):
                    if act is not None:
                        act.wait_ge(s["w_ld"], 16 * (2 * layer + k + 1))
                        nc.scalar.activation(dst[:, 0], stage[:, :, :], ACT.Copy).then_inc(s["w_hi"], 1)
                    else:
                        dve.wait_ge(s["w_hi"], 2 * layer + k + 1)
                        nc.vector.tensor_tensor(dst[:, 1], stage[:, :, :], dst[:, 0], ALU.subtract).then_inc(s["w_lo"], 1)

            def pe_prog(pe):
                pe.wait_ge(m["phase_end"], base)
                pe.wait_ge(s["w_lo"], 2 * layer + 2)

                def up_products(i, e, u):
                    for c in range(C):
                        wait(pe, evs[c], u)
                        for k, (a, w) in enumerate(((0, 0), (1, 0), (0, 1))):
                            mm = nc.tensor.matmul(ps_s[:, c, :], up_hl[:, w, e, c * 128:(c + 1) * 128],
                                                  xt_hl[:, a, bass.ds((i - o) * TOK, TOK)], start=k == 0, stop=k == 2)
                        mm.then_inc(ups[c], 1)

                def down_products(e, u):
                    ps = (ps_a, ps_b)[e % 2]
                    pe.wait_ge(los[C - 1], u + 1)
                    wait(pe, s["x_new"], u - 1)
                    for b in range(TB):
                        o_ = ps[:, b * 128:(b + 1) * 128]
                        if layer:
                            nc.tensor.matmul(o_, ones_bf[:, :], bias_bf[:, B2 + e * D:B2 + (e + 1) * D], start=True, stop=False)
                        for c in range(C):
                            for k, (a, w) in enumerate(((0, 0), (0, 1), (1, 0))):
                                mm = nc.tensor.matmul(o_, h_hl[:, e % 2, a, c, b * 128:(b + 1) * 128], down_hl[:, w, e, c, :],
                                                      start=not layer and c == 0 and k == 0, stop=c == C - 1 and k == 2)
                    mm.then_inc(s["y"], 1)

                up_products(o, 0, o * E)
                for e in range(E):
                    if e < E - 1:
                        up_products(o, e + 1, o * E + e + 1)
                    else:
                        up_products(o + 1, 0, o * E + E)
                    down_products(e, o * E + e)
                with pe.Fori(o + 1, o + NBLK - 1) as i:
                    for e in range(E):
                        if e < E - 1:
                            up_products(i, e + 1, i * E + e + 1)
                        else:
                            up_products(i + 1, 0, i * E + E)
                        down_products(e, i * E + e)
                i = o + NBLK - 1
                for e in range(E):
                    if e < E - 1:
                        up_products(i, e + 1, i * E + e + 1)
                    down_products(e, i * E + e)
                phase_end(pe)

            def act_prog(act):
                act.wait_ge(m["phase_end"], base)
                split_weights(act, None)
                with act.Fori(o, o + NBLK) as i:
                    for e in range(E):
                        u = i * E + e
                        for c in range(C):
                            act.wait_ge(ups[c], u + 1)
                            act.wait_ge(los[c], u)
                            if layer:
                                nc.scalar.activation(h32[:, c, :], ps_s[:, c, :], ACT.Relu, bias=b1_f[:, e, c:c + 1]).then_inc(evs[c], 1)
                            else:
                                nc.scalar.activation(h32[:, c, :], ps_s[:, c, :], ACT.Gelu_apprx_tanh).then_inc(evs[c], 1)
                phase_end(act)

            def pool_prog(pool):
                pool.wait_ge(m["phase_end"], base)
                phase_end(pool)

            def dve_prog(dve):
                dve.wait_ge(m["phase_end"], base)
                split_weights(None, dve)

                def hidden(e, u):
                    for c in range(C):
                        dve.wait_ge(evs[c], u + 1)
                        if c == 0:
                            wait(dve, s["y"], u - 1)
                        nc.vector.tensor_copy(h_hl[:, e % 2, 0, c, :], h32[:, c, :]).then_inc(his[c], 1)
                        dve.wait_ge(his[c], u + 1)
                        nc.vector.tensor_tensor(h_hl[:, e % 2, 1, c, :], h32[:, c, :], h_hl[:, e % 2, 0, c, :], ALU.subtract).then_inc(los[c], 1)

                def residual(i, e, u):
                    ps = (ps_a, ps_b)[e % 2]
                    dve.wait_ge(s["y"], u + 1)
                    wait(dve, s["x_new"], u)
                    for b in range(TB):
                        xb = x_all[:, bass.ds((i - o) * TB + b, 1), :].rearrange("s b d -> s (b d)")
                        gb = gate[:, bass.ds((i - o) * TB + b, 1), e:e + 1].rearrange("s b e -> s (b e)")
                        ins = nc.vector.scalar_tensor_tensor(xb, ps[:, b * 128:(b + 1) * 128], gb, xb, ALU.mult, ALU.add)
                    ins.then_inc(s["x_new"], 1)

                hidden(0, o * E)
                for e in range(E):
                    hidden((e + 1) % 2, o * E + e + 1)
                    residual(o, e, o * E + e)
                with dve.Fori(o + 1, o + NBLK - 1) as i:
                    for e in range(E):
                        hidden((e + 1) % 2, i * E + e + 1)
                        residual(i, e, i * E + e)
                i = o + NBLK - 1
                for e in range(E):
                    if e < E - 1:
                        hidden((e + 1) % 2, i * E + e + 1)
                    residual(i, e, i * E + e)
                phase_end(dve)

            progs["sp"].append(sp_prog)
            progs["pool"].append(pool_prog)
            progs["pe"].append(pe_prog)
            progs["act"].append(act_prog)
            progs["dve"].append(dve_prog)

        for layer in range(2):
            attention(layer)
            experts(layer)

        def store(sp):
            sp.wait_ge(m["phase_end"], 4 * 4)
            for k in range(8):
                sp.dma_start(out[k * 8:(k + 1) * 8].rearrange("b s d -> s b d"), x_all[:, k * 8:(k + 1) * 8, :]).then_inc(m["out_st"], 16)
            sp.wait_ge(m["out_st"], 128)

        @block.sync
        def _(sp):
            for f in progs["sp"]:
                f(sp)
            store(sp)

        @block.gpsimd
        def _(pool):
            for f in progs["pool"]:
                f(pool)

        @block.scalar
        def _(act):
            for f in progs["act"]:
                f(act)

        @block.vector
        def _(dve):
            for f in progs["dve"]:
                f(dve)

        @block.tensor
        def _(pe):
            for f in progs["pe"]:
                f(pe)


def kernel(**inputs):
    import numpy as np
    import concourse.bacc as bacc
    from concourse import mybir
    from concourse.bass_utils import run_bass_kernel_spmd

    a = {k: np.ascontiguousarray(v) for k, v in inputs.items()}

    def stack(w, rows):
        w = w.reshape((G, 4, 1, HD) + w.shape[1:])
        full = np.zeros((G, 4, 4, HD) + w.shape[4:], w.dtype)
        full[:, :, 0:3] = w
        return full.reshape((G * 128,) + w.shape[4:])

    def stacks(name):
        both = [stack(a[f"L{l}_xattn_{name}"], G).T.reshape(D, G, 128) for l in range(2)]
        return np.ascontiguousarray(np.stack(both, 1))

    def both_t(name):
        return np.ascontiguousarray(np.stack([a[f"L{l}_xattn_{name}"].T for l in range(2)], 1))

    bias = np.concatenate([
        stack(a["L1_xattn_bq"], 0), stack(a["L1_xattn_bk"], 0), a["L1_xattn_bv"], a["L1_xattn_bo"], a["L0_xattn_bo"],
        a["L1_ffn_b2"].reshape(-1), a["L1_ffn_rb2"]])
    row = np.arange(128)
    consts = np.zeros((128, NCONST), np.float32)
    consts[:, C_ID:C_ID + 128] = np.eye(128)
    consts[:, C_NQ] = np.where(row // HD % 4 == 2, -1, 0)
    consts[:, C_NK] = np.where(row // HD % 4 == 1, -1, 0)
    consts[0:3, C_SEL:C_SEL + 3] = np.eye(3)
    consts[:, C_HALF:C_HALF + TB] = -0.5
    consts[:, C_EPS:C_EPS + TB] = EPS
    consts[:, C_UP:C_UP + 64] = np.triu(np.ones((E, E)), 1).reshape(-1)
    consts[:, C_LOW:C_LOW + 64] = np.tril(np.ones((E, E)), -1).reshape(-1)
    small = np.concatenate([
        a["L0_ffn_router_w"], a["L1_ffn_rw1"], a["L1_ffn_rw2"].reshape(C, 128, E).transpose(1, 0, 2).reshape(128, -1),
        a["L1_ffn_b1"].reshape(E, C, 128).transpose(2, 0, 1).reshape(128, -1), a["L1_ffn_rb1"].reshape(C, 128).T], 1)
    up = np.stack([a["L0_ffn_up_w"].transpose(1, 0, 2), a["L1_ffn_W1"].transpose(1, 0, 2)])
    down = np.stack([a[n].reshape(E, C, 128, D).transpose(2, 0, 1, 3).reshape(128, E, C * D) for n in ("L0_ffn_down_w", "L1_ffn_W2")])
    arrays = {
        "x": a["x"], "ctx": a["ctx_1024"], "mask0": a["mask_Bx1xSxS2_if1"], "mask1": a["mask_BxS2_ff1"],
        "gates": np.concatenate([a["g_xattn"], a["g_ffn"]]), "consts": consts,
        "wq": stacks("Wq"), "wk": stacks("Wk"), "wv": both_t("Wv"), "wo": both_t("Wo"),
        "biases": np.ascontiguousarray(np.broadcast_to(bias, (3, NBIAS))), "small": small,
        "up": np.ascontiguousarray(up), "down": np.ascontiguousarray(down),
    }
    nc = bacc.Bacc("TRN2", target_bir_lowering=False, num_devices=1)
    t = {k: nc.dram_tensor(f"in_{k}", v.shape, mybir.dt.from_np(v.dtype), kind="ExternalInput").ap() for k, v in arrays.items()}
    out = nc.dram_tensor("out_0", (B, S, D), mybir.dt.float32, kind="ExternalOutput").ap()
    flamingo(nc, t["x"], t["ctx"], t["mask0"], t["mask1"], t["gates"], t["consts"], t["wq"], t["wk"], t["wv"], t["wo"],
             t["biases"], t["small"], t["up"], t["down"], None, None, None, None, out)
    r = run_bass_kernel_spmd(nc, [{f"in_{k}": np.ascontiguousarray(v) for k, v in arrays.items()}], core_ids=[0])
    return r.results[0]["out_0"]
```

```python
from contextlib import ExitStack

import numpy as np

import concourse.bass as bass
from concourse import mybir

F32 = mybir.dt.float32
F16 = mybir.dt.float16
BF16 = mybir.dt.bfloat16
I32 = mybir.dt.int32
ALU = mybir.AluOpType
ACT = mybir.ActivationFunctionType
AX = mybir.AxisListType.X

B, S, D = 64, 128, 128
K2 = 77
H, HD = 16, 8
G = 4
E, HID = 8, 512
C = HID // 128
TB = 4
NBLK = B // TB
TOK = TB * S
TOPK = (4, 2)
CAP = B * S + TOK
TILES = tuple(-(-(k * B * S // TOK + E - 1) // 2) * 2 for k in TOPK)
MAXT = max(TILES)
FREE = 320
INV = 1.0 / np.sqrt(np.float32(HD))
PEN0 = float(-1e20 * INV)
FMIN = float(np.finfo(np.float32).min)
EPS = 1e-5

BQ, BK, BV, BO1, BO0, B2, RB2 = 0, 512, 1024, 1152, 1280, 1408, 1408 + E * D
NBIAS = RB2 + E
C_ID, C_NQ, C_NK, C_SEL, C_LOW, C_HALF, C_EPS = 0, 128, 129, 130, 133, 197, 201
C_TRI = C_EPS + TB
C_K = C_TRI + 128
C_J = C_K + TOPK[0] * E
C_TAU = C_J + B * S // TOK
C_ROW0 = C_TAU + MAXT
NCONST = C_ROW0 + E


def wait(eng, sem, value):
    if isinstance(value, int) and value <= 0:
        return
    eng.wait_ge(sem, value)


def loaded(i, p):
    return 8 * (i - p) + 16


def flamingo(nc, x, ctx_in, mask0, mask1, gates_in, consts, wq, wk, wv, wo, biases, small, weights, out, xs, ys):
    with ExitStack() as ctx:
        def sb(name, shape, dt):
            return ctx.enter_context(nc.sbuf_tensor(name, shape, dt))

        def sem(name):
            return ctx.enter_context(nc.semaphore(name))

        made = {}

        def shared_sem(name):
            if name not in made:
                made[name] = sem(name)
            return made[name]

        x_all = sb("x_all", [128, B, D], F32)
        cst = sb("cst", [128, NCONST], F32)
        ident_bf = sb("ident_bf", [128, 128], BF16)
        ones_all = sb("ones_all", [128, 128], BF16)
        ones_bf = ones_all[0:3, :]
        full_bf = sb("full_bf", [128, 128], BF16)
        tri_bf = sb("tri_bf", [128, 128], BF16)
        tg = sb("tg", [128, 4], F32)
        wq_s = sb("wq_s", [128, 2, G, 128], F32)
        wk_s = sb("wk_s", [128, 2, G, 128], F32)
        wv_s = sb("wv_s", [128, 2, 128], F32)
        wo_s = sb("wo_s", [128, 2, 128], F32)
        bias_bf = sb("bias_bf", [3, NBIAS], BF16)
        pen_f = sb("pen_f", [B, 4, K2], F32)
        pen_parts = sb("pen_parts", [B, 3, K2], BF16)
        pen1 = sb("pen1", [128, B, K2], BF16)
        stage = sb("stage", [128, HID], F32)
        w_hl = sb("w_hl", [128, 2, 2 * E, HID], F16)
        up_hl = w_hl[:, :, 0:E, :]
        down_hl = w_hl[:, :, E:2 * E, :].rearrange("p t e (c d) -> p t e c d", c=C)
        small_w = sb("small_w", [128, E + HID + C * E + E * C + C], F32)
        rw0_hl = sb("rw0_hl", [128, 2, E], F16)
        rw1_hl = sb("rw1_hl", [128, 2, HID], F16)
        rw2_hl = sb("rw2_hl", [128, 2, C, E], F16)
        ctx_s = sb("ctx_s", [K2, 2, D], F32)
        mask_s = sb("mask_s", [128, 2, K2], I32)
        pen0 = sb("pen0", [128, 2, K2], BF16)
        stats = sb("stats", [128, 2, 6], F32)
        mv = sb("mv", [128, 2, 2], F32)
        rstd = sb("rstd", [128, 2, 1], F32)
        xn = sb("xn", [128, 2, D], F32)
        xc_t = sb("xc_t", [128, 2, 128 + K2], F32)
        at = sb("at", [128, 128], F32)
        q_hi = sb("q_hi", [128, G, 128], F16)
        q_st = sb("q_st", [128, G, 128], F16)
        k_hi = sb("k_hi", [128, G, K2], F16)
        k_st = sb("k_st", [128, G, K2], F16)
        v_s = sb("v_s", [K2, TB, H, 32], F32)
        mx = sb("mx", [128, H], F32)
        sd = sb("sd", [128, 4, G, K2], F32)
        NP, NPT = H * K2, H * 128
        shared = sb("shared", [128, max(NP + NPT, 2 * C * TOK)], F32)
        p_s = shared[:, 0:NP].rearrange("q (j g k) -> q j g k", j=4, g=G)
        pt_s = shared[0:K2, NP:NP + NPT].rearrange("k (j g q) -> k j g q", j=4, g=G)
        u_s = sb("u_s", [128, G, 128], F32)
        rden = sb("rden", [128, H], F32)
        an = sb("an", [128, H, HD], F32)
        xn4 = sb("xn4", [128, TB, D], F32)
        hr_hl = sb("hr_hl", [128, 2, C, 128], F16)
        wide = sb("wide", [128, B * S], F32)
        xt_hl = wide[:, 0:TOK].bitcast(F16).rearrange("p (a n) -> p a n", a=2)
        xg = wide[:, TOK:3 * TOK].rearrange("p (a n) -> p a n", a=2)
        xt2 = wide[:, 3 * TOK:5 * TOK].bitcast(F16).rearrange("p (a t n) -> p a t n", a=2, t=2)
        y_s = wide[:, 5 * TOK:7 * TOK].rearrange("p (a n) -> p a n", a=2)
        yg = wide[:, 7 * TOK:9 * TOK].rearrange("p (a d) -> p a d", d=D)
        zeros = wide[:, 9 * TOK:10 * TOK]
        xsc = wide[:, 10 * TOK:11 * TOK].rearrange("p (b d) -> p b d", b=TB)
        bias_f = wide[0:3, 0:3 * NBIAS].rearrange("p (a n) -> p a n", a=3)
        h32 = sb("h32", [128, C, TOK], F32)
        h_hl = shared[:, 0:2 * C * TOK].bitcast(F16).rearrange("p (a t c n) -> p a t c n", a=2, t=2, c=C)
        lg = sb("lg", [128, TB, E], F32)
        cmp_a = sb("cmp_a", [128, TB, E, E], F32)
        cmp_b = sb("cmp_b", [128, TB, E, E], F32)
        rank = sb("rank", [128, TB, E], F32)
        lmax = sb("lmax", [128, TB], F32)
        lsum = sb("lsum", [128, TB], F32)
        gate = sb("gate", [128, TB, E], F32)
        sel_bf = sb("sel_bf", [128, TB + 1, E], BF16)
        row_end = sb("row_end", [128, E], F32)
        pos = sb("pos", [128, TB, E], F32)
        is_k = sb("is_k", [128, TB, TOPK[0], E], F32)
        pick = sb("pick", [128, TB, TOPK[0], E], F32)
        pick2 = sb("pick2", [128, TB, TOPK[0], E], F32)
        idx_f = sb("idx_f", [128, TB, TOPK[0]], F32)
        idx4 = sb("idx4", [128, TB, TOPK[0]], I32)
        row_all = sb("row_all", [128, B, TOPK[0]], F32)
        idx_all = sb("idx_all", [128, B, TOPK[0]], I32)
        y_off = wide[:, 11 * TOK + 2 * MAXT * E:11 * TOK + 2 * MAXT * E + B * TOPK[0]].rearrange("p (b k) -> p b k", b=B)
        stat_all = sb("stat_all", [128, B, 2], F32)
        xc4 = sb("xc4", [128, TB, D], F32)
        junk = sb("junk", [128, 1], F32)
        spare = sb("spare", [128, 10], F32)
        idx_g = sb("idx_g", [128, 4 * TB, TOPK[0]], I32)
        gk_all = sb("gk_all", [128, B, TOPK[0]], F32)
        t_cnt = sb("t_cnt", [128, E], F32)
        t_gt = sb("t_gt", [128, E, B * S // TOK], F32)
        t_n = sb("t_n", [128, E], F32)
        t_low = sb("t_low", [1, E, E], F32)
        t_first = sb("t_first", [1, E], F32)
        t_last = sb("t_last", [1, 1], F32)
        t_tau = sb("t_tau", [1, MAXT], F32)
        t_ge, t_mul = (wide[0:1, at:at + MAXT * E].rearrange("p (t e) -> p t e", e=E) for at in (11 * TOK, 11 * TOK + MAXT * E))
        t_step = sb("t_step", [128, E], F32)
        t_row = sb("t_row", [1, MAXT], F32)
        end_i = sb("end_i", [1, E], I32)
        tab_e = sb("tab_e", [1, MAXT], I32)
        tab_row = sb("tab_row", [1, MAXT], I32)

        ps_s = ctx.enter_context(nc.psum_tensor("ps_s", [128, 4, 512], F32))
        ps_a = ctx.enter_context(nc.psum_tensor("ps_a", [128, 512], F32))
        ps_b = ctx.enter_context(nc.psum_tensor("ps_b", [128, 512], F32))
        ps_6 = ctx.enter_context(nc.psum_tensor("ps_6", [128, 512], F32))
        ps_7 = ctx.enter_context(nc.psum_tensor("ps_7", [128, 512], F32))

        ident = cst[:, C_ID:C_ID + 128]

        def carry_waits(k):
            nc.gpsimd.tensor_tensor(spare[:, k:k + 1], cst[:, C_EPS:C_EPS + 1], cst[:, C_EPS:C_EPS + 1], ALU.add)

        names = ("setup_ld", "const_ok", "bias_ok", "pen_moved", "phase_end", "setup_chain", "out_st")
        m = {n: sem(n) for n in names}
        block = ctx.enter_context(nc.Block())
        progs = {k: [] for k in ("sp", "act", "dve", "pool", "pe")}

        def setup_sp(sp):
            sp.dma_start(cst[:, :], consts).then_inc(m["setup_ld"], 16)
            sp.dma_start(tg[:, :], gates_in.partition_broadcast(128)).then_inc(m["setup_ld"], 16)
            sp.dma_start(wq_s[:, :, :, :], wq).then_inc(m["setup_ld"], 16)
            sp.dma_start(wk_s[:, :, :, :], wk).then_inc(m["setup_ld"], 16)
            sp.dma_start(wv_s[:, :, :], wv).then_inc(m["setup_ld"], 16)
            sp.dma_start(wo_s[:, :, :], wo).then_inc(m["setup_ld"], 16)
            sp.dma_start(bias_f[:, 0, :], biases).then_inc(m["setup_ld"], 16)
            sp.dma_start(pen_f[:, 0, :], mask1).then_inc(m["setup_ld"], 16)
            sp.dma_start(small_w[:, :], small).then_inc(m["setup_ld"], 16)

        NLD = 16 * 9
        o = 0
        rw0_f = small_w[:, o:o + E]; o += E
        rw1_f = small_w[:, o:o + HID]; o += HID
        rw2_f = small_w[:, o:o + C * E].rearrange("p (c e) -> p c e", c=C); o += C * E
        b1_f = small_w[:, o:o + E * C].rearrange("p (e c) -> p e c", e=E); o += E * C
        rb1_f = small_w[:, o:o + C]

        def setup_pool(pool):
            nc.gpsimd.memset(v_s[:, :, :, :], 0.0).then_inc(m["setup_chain"], 1)
            nc.gpsimd.memset(ones_all[:, :], 0.0).then_inc(m["setup_chain"], 1)
            nc.gpsimd.memset(pen1[:, :, :], 0.0).then_inc(m["const_ok"], 1)
            nc.gpsimd.memset(full_bf[:, :], 1.0).then_inc(m["const_ok"], 1)
            nc.gpsimd.memset(sel_bf[:, TB, :], 0.0).then_inc(m["const_ok"], 1)
            pool.wait_ge(m["setup_chain"], 2)
            nc.gpsimd.memset(ones_bf[:, :], 1.0).then_inc(m["const_ok"], 1)
            nc.gpsimd.memset(v_s[:, :, :, HD:HD + 1], 1.0).then_inc(m["const_ok"], 1)
            pool.wait_ge(m["setup_ld"], NLD)
            nc.gpsimd.tensor_copy(ident_bf[:, :], ident).then_inc(m["const_ok"], 1)
            nc.gpsimd.tensor_copy(tri_bf[:, :], cst[:, C_TRI:C_TRI + 128]).then_inc(m["const_ok"], 1)

        def setup_act(act):
            act.wait_ge(m["setup_ld"], NLD)
            nc.scalar.activation(tg[:, :], tg[:, :], ACT.Tanh).then_inc(m["const_ok"], 1)

        def parts(dve, v, chain):
            mask = -65536
            for k in range(1, 3):
                chain(nc.vector.tensor_single_scalar(v[:, k].bitcast(I32), v[:, 0].bitcast(I32), mask, op=ALU.bitwise_and))
                chain(nc.vector.tensor_tensor(v[:, 0], v[:, 0], v[:, k], ALU.subtract))
            chain(nc.vector.tensor_copy(v[:, 3], v[:, 0]))

        def setup_dve(dve):
            count = [0]
            chain_sem = m["bias_ok"]

            def chain(ins):
                count[0] += 1
                ins.then_inc(chain_sem, 1)
                dve.wait_ge(chain_sem, count[0])

            dve.wait_ge(m["setup_ld"], NLD)
            nc.vector.tensor_scalar(wq_s[:, :, :, :], wq_s[:, :, :, :], float(INV), None, ALU.mult).then_inc(m["const_ok"], 1)
            v, part, kept = bias_f[:, 0], bias_f[:, 1], bias_f[:, 2]
            sel = cst[0:3, C_SEL:C_SEL + 3]
            chain(nc.vector.tensor_scalar(v[:, BQ:BQ + 512], v[:, BQ:BQ + 512], float(INV), None, ALU.mult))
            chain(nc.vector.tensor_single_scalar(part.bitcast(I32), v.bitcast(I32), -65536, op=ALU.bitwise_and))
            chain(nc.vector.tensor_tensor(v, v, part, ALU.subtract))
            chain(nc.vector.tensor_scalar(kept, part, sel[:, 0:1], None, ALU.mult))
            chain(nc.vector.tensor_single_scalar(part.bitcast(I32), v.bitcast(I32), -65536, op=ALU.bitwise_and))
            chain(nc.vector.tensor_tensor(v, v, part, ALU.subtract))
            chain(nc.vector.scalar_tensor_tensor(kept, part, sel[:, 1:2], kept, ALU.mult, ALU.add))
            chain(nc.vector.scalar_tensor_tensor(bias_bf[:, :], v, sel[:, 2:3], kept, ALU.mult, ALU.add))
            chain(nc.vector.tensor_scalar(pen_f[:, 0, :], pen_f[:, 0, :], -1.0, 1.0, ALU.mult, ALU.add))
            chain(nc.vector.tensor_scalar(pen_f[:, 0, :], pen_f[:, 0, :], FMIN, None, ALU.mult))
            parts(dve, pen_f, chain)
            chain(nc.vector.tensor_copy(pen_parts[:, :, :], pen_f[:, 1:4, :]))
            for k, (hl, w) in enumerate(((rw0_hl, rw0_f), (rw1_hl, rw1_f), (rw2_hl, rw2_f))):
                chain(nc.vector.tensor_copy(hl[:, 0], w))
                chain(nc.vector.tensor_tensor(hl[:, 1], w, hl[:, 0], ALU.subtract))
            assert count[0] == BIAS_STEPS

        BIAS_STEPS = 8 + 2 + 5 + 1 + 6
        NCONST_OK = 9

        def pen_sp(sp):
            sp.wait_ge(m["bias_ok"], BIAS_STEPS)
            sp.wait_ge(m["const_ok"], NCONST_OK)
            for k in range(3):
                sp.dma_start(pen1[k:k + 1, :, :], pen_parts[:, k, :]).then_inc(m["pen_moved"], 16)

        def attention(layer):
            o = layer * B
            n = ("x_ld0", "x_ld1", "ctx_ld0", "ctx_ld1", "mask_ld0", "mask_ld1", "pen", "st1", "st2", "st3", "st4", "xn", "xct", "xct_ev", "q", "q_hi", "q_st",
                 "kv", "v_ev", "k_hi", "k_st", "s", "mx", "sd", "p", "pt0", "pt1", "pt2", "pt3", "pe0", "pe1", "pe2", "pe3",
                 "u", "u_ev", "ut", "rden", "an", "a_t", "at_ev", "o", "x_new")
            s = {k: shared_sem("a_" + k) for k in n}
            neg_q, neg_k = cst[:, C_NQ:C_NQ + 1], cst[:, C_NK:C_NK + 1]

            K = TOPK[layer]
            CHAIN = 13 if layer else 9
            SORT = 14 if layer else 11
            PLACE = 15 if layer else 11
            rn = ("st", "st2", "st3", "st4", "xn", "xt", "hi", "lo", "hid", "h_ev", "h_hi", "h_lo", "l", "lg", "lmax", "sub", "exp",
                  "cmp", "cmq", "cms", "rank", "sel", "prod", "sum", "rec", "gate", "pos", "pos_ev", "end", "is_k", "pick", "idx_f", "idx", "gk", "xsc", "stat", "centred", "sorted",
                  "idx_g", "combined", "g_ld0", "g_ld1", "w_ld", "w_hi", "w_lo")
            z = {k: shared_sem("r_" + k) for k in rn}
            OR = layer * NBLK

            def xct_of(i):
                return i + 1

            def on(i):
                return not isinstance(i, int) or o <= i < o + B

            def block_on(r):
                return not isinstance(r, int) or OR <= r < OR + NBLK

            def due(r, b, step):
                return b == step % TB and block_on(r - step // TB)

            def sorted_count(R):
                return 16 * TB * (K * (R - OR) + layer * TOPK[0] * NBLK)

            def token_rows(R, b):
                return x_all[:, bass.ds((R - OR) * TB + b, 1), :].rearrange("s b d -> s (b d)")

            def steps(eng, f):
                for r in (0, 1, 2):
                    for b in range(TB):
                        f(eng, OR + r, b)
                with eng.Fori(OR + 3, OR + NBLK - 1) as r:
                    for b in range(TB):
                        f(eng, r, b)
                for r in (NBLK - 1, NBLK, NBLK + 1, NBLK + 2):
                    for b in range(TB):
                        f(eng, OR + r, b)

            def load(sp, i, p):
                if layer == 0:
                    wait(sp, s["st1"], i - 1)
                    sp.dma_start(x_all[:, bass.ds(i - o, 1), :], x[bass.ds(i - o, 1), :, :].rearrange("b s d -> s b d")).then_inc(s[f"x_ld{p}"], 16)
                wait(sp, s["xct"], xct_of(i - 2))
                sp.dma_start(ctx_s[:, p, :], ctx_in[bass.ds(i - o, 1), :, :].rearrange("b s d -> s (b d)")).then_inc(s[f"ctx_ld{p}"], 16)
                if layer == 0:
                    wait(sp, s["pen"], i - 1)
                    sp.dma_start(mask_s[:, p, :], mask0[bass.ds(i - o, 1), 0, :, :].rearrange("b s k -> s (b k)")).then_inc(s[f"mask_ld{p}"], 16)

            def sp_prog(sp):
                if layer == 0:
                    setup_sp(sp)
                else:
                    sp.wait_ge(m["phase_end"], 2 * 4)
                load(sp, o, 0)
                load(sp, o + 1, 1)
                if layer == 0:
                    pen_sp(sp)
                with sp.Fori(o + 2, o + B - 1, 2) as i:
                    load(sp, i, 0)
                    load(sp, i + 1, 1)

            def pool_batch(pool, i, p):
                if layer == 0:
                    wait(pool, s[f"mask_ld{p}"], loaded(i, p))
                    wait(pool, s["s"], i - 1)
                wait(pool, s["st2"], i + 1)
                nc.gpsimd.tensor_tensor(rstd[:, p, :], mv[:, p, 1:2], cst[:, C_EPS:C_EPS + 1], ALU.add).then_inc(s["st3"], 1)
                if layer == 0:
                    nc.gpsimd.tensor_scalar(pen0[:, p, :], mask_s[:, p, :], 0, PEN0, ALU.is_equal, ALU.mult).then_inc(s["pen"], 1)
                wait(pool, s["st3"], i + 1)
                nc.gpsimd.tensor_tensor(rstd[:, p, :], rstd[:, p, :], cst[:, C_HALF:C_HALF + 1], ALU.pow).then_inc(s["st4"], 1)

            def pool_step(pool, r, b):
                i = r * TB + b
                if on(i + 2):
                    pool_batch(pool, i + 2, b % 2)
                if layer and on(i + 4):
                    gather(pool, i + 4, b % 2)
                if b == 2 and block_on(r - 1):
                    R = r - 1
                    pool.wait_ge(z["st2"], R + 1)
                    nc.gpsimd.tensor_tensor(rs4[:, :, 0], mv4[:, :, 1], cst[:, C_EPS:C_EPS + TB], ALU.add).then_inc(z["st3"], 1)
                    pool.wait_ge(z["st3"], R + 1)
                    nc.gpsimd.tensor_tensor(rs4[:, :, 0], rs4[:, :, 0], cst[:, C_HALF:C_HALF + TB], ALU.pow).then_inc(z["st4"], 1)
                for b_ in range(TB):
                    step = PLACE + (0 if layer else b_ // 2)
                    if due(r, b, step):
                        R = r - step // TB
                        if b_ == 0:
                            pool.wait_ge(z["xsc"], R + 1)
                            pool.wait_ge(z["idx"], R + 1)
                            carry_waits(6 + R % 4 if isinstance(R, int) else 1)
                        for k in range(K):
                            nc.gpsimd.indirect_dma_start(xs, bass.IndirectOffsetOnAxis(ap=idx4[:, b_, k:k + 1], axis=0),
                                                         xsc[:, b_, :], None).then_inc(z["sorted"], 16)

            def gather(pool, j, p):
                wait(pool, z["combined"], TOPK[0] * (j - o - 1))
                carry_waits(2)
                nc.gpsimd.tensor_copy(idx_g[:, p:p + 1, :], idx_all[:, bass.ds(j - o, 1), :]).then_inc(z["idx_g"], 1)
                pool.wait_ge(z["idx_g"], j - o + 1)
                carry_waits(3)
                for k in range(TOPK[0]):
                    nc.gpsimd.indirect_dma_start(yg[:, p * TOPK[0] + k, :], None, ys,
                                                 bass.IndirectOffsetOnAxis(ap=idx_g[:, p, k:k + 1], axis=0)).then_inc(z[f"g_ld{p}"], 16)

            def pool_prog(pool):
                if layer == 0:
                    setup_pool(pool)
                else:
                    pool.wait_ge(m["phase_end"], 2 * 4)
                    pool.wait_ge(shared_sem("f_y_st"), 16 * TILES[0])
                    for j in range(4):
                        gather(pool, o + j, j % 2)
                pool_batch(pool, o, 0)
                pool_batch(pool, o + 1, 1)
                steps(pool, pool_step)
                phase_end(pool)

            def next_transposes(pe, i, p):
                pe.wait_ge(s["xn"], i + 1)
                pe.wait_ge(s[f"ctx_ld{p}"], loaded(i, p))
                nc.tensor.transpose(ps_7[:, 0:128], xn[:, p, :], ident)
                return nc.tensor.transpose(ps_7[:, 128:128 + K2], ctx_s[:, p, :], ident[0:K2, 0:K2])

            def prob_transposes(j, sem_):
                ps = (ps_a, ps_b)[j % 2]
                for g in range(G):
                    mm = nc.tensor.transpose(ps[0:K2, g * 128:(g + 1) * 128], p_s[:, j, g, :], ident)
                mm.then_inc(sem_, 1)

            def token_transposes(pe, R):
                pe.wait_ge(z["xn"], R + 1)
                for b in range(TB):
                    mm = nc.tensor.transpose(ps_a[:, b * 128:(b + 1) * 128], xn4[:, b, :], ident)
                mm.then_inc(z["xt"], 1)

            def router_hidden(pe, R, b):
                for c in range(C):
                    for k, (a, w) in enumerate(((0, 0), (1, 0), (0, 1))):
                        mm = nc.tensor.matmul(ps_b[:, c * 128:(c + 1) * 128], rw1_hl[:, w, c * 128:(c + 1) * 128],
                                              xt_hl[:, a, b * 128:(b + 1) * 128], start=k == 0, stop=k == 2)
                mm.then_inc(z["hid"], 1)

            def router_logits(pe, R, b):
                o_ = ps_s[:, 0, FREE + 128 + b * E:FREE + 128 + (b + 1) * E]
                if layer == 0:
                    for k, (a, w) in enumerate(((0, 0), (0, 1), (1, 0))):
                        mm = nc.tensor.matmul(o_, xt_hl[:, a, b * 128:(b + 1) * 128], rw0_hl[:, w, :],
                                              start=k == 0, stop=k == 2)
                else:
                    pe.wait_ge(z["h_lo"], R * TB - o + b + 1)
                    nc.tensor.matmul(o_, ones_bf[:, :], bias_bf[:, RB2:RB2 + E], start=True, stop=False)
                    for c in range(C):
                        for k, (a, w) in enumerate(((0, 0), (0, 1), (1, 0))):
                            mm = nc.tensor.matmul(o_, hr_hl[:, a, c, :], rw2_hl[:, w, c, :], start=False, stop=c == C - 1 and k == 2)
                mm.then_inc(z["l"], 1)

            def place(pe, R, i):
                pe.wait_ge(z["sel"], R + 1)
                if on(i + 1):
                    pe.wait_ge(s["xct_ev"], xct_of(i + 1))
                else:
                    pe.wait_ge(s["x_new"], min(i - 2, o + B))
                nc.tensor.matmul(ps_7[:, 0:(TB + 1) * E], tri_bf[:, :], sel_bf[:, :, :].rearrange("p b e -> p (b e)"), start=True, stop=True)
                for b_ in range(TB):
                    mm = nc.tensor.matmul(ps_7[:, (b_ + 1) * E:(TB + 1) * E].rearrange("p (b e) -> p b e", e=E), full_bf[:, :],
                                          sel_bf[:, b_:b_ + 1, :].broadcast_to([128, TB - b_, E]),
                                          start=False, stop=True, skip_group_check=True)
                mm.then_inc(z["pos"], 1)

            def pe_step(pe, r, b):
                i = r * TB + b
                p = b % 2
                t, w = i - 2, i - 3
                if on(w):
                    pe.wait_ge(s["u_ev"], w + 1)
                    pe.wait_ge(s["xct_ev"], xct_of(min(i, o + B - 1) if isinstance(i, int) else i))
                    if due(r, b, PLACE):
                        pe.wait_ge(z["end"], r - PLACE // TB + 1)
                    wait(pe, s["x_new"], w)
                    for g in range(G):
                        mm = nc.tensor.transpose(ps_7[:, g * 128:(g + 1) * 128], u_s[:, g, :], ident)
                    mm.then_inc(s["ut"], 1)
                if on(i):
                    pe.wait_ge(s["xct_ev"], xct_of(i))
                    wait(pe, s["k_st"], i)
                    for g in range(G):
                        o_ = ps_6[:, g * 128:(g + 1) * 128]
                        mm = nc.tensor.matmul(o_, wq_s[:, layer, g, :], xc_t[:, p, 0:128], start=True, stop=layer == 0)
                        if layer:
                            mm = nc.tensor.matmul(o_, bias_bf[:, BQ + g * 128:BQ + (g + 1) * 128], ones_bf[:, :], start=False, stop=True)
                    mm.then_inc(s["q"], 1)
                if due(r, b, 8):
                    pe.wait_ge(z["lo"], r - 1)
                if layer:
                    for b_ in range(TB):
                        if due(r, b, 9 + b_):
                            pe.wait_ge(z["h_ev"], (r - (9 + b_) // TB) * TB - o + b_ + 1)
                if on(t):
                    pe.wait_ge(s["p"], t + 1)
                    prob_transposes(0, s["pt0"])
                    prob_transposes(1, s["pt1"])
                if on(w):
                    pe.wait_ge(s["an"], w + 1)
                    nc.tensor.transpose(ps_7[:, 0:128], an[:, :, :].rearrange("q h d -> q (h d)"), ident).then_inc(s["a_t"], 1)
                if on(t):
                    for j in (2, 3):
                        pe.wait_ge(s[f"pe{j - 2}"], t + 1)
                        prob_transposes(j, s[f"pt{j}"])
                if on(w):
                    pe.wait_ge(s["at_ev"], w + 1)
                    nc.tensor.matmul(ps_7[:, 0:128], at[:, :], wo_s[:, layer, :], start=True, stop=False)
                    bo = BO1 if layer else BO0
                    nc.tensor.matmul(ps_7[:, 0:128], ones_bf[:, :], bias_bf[:, bo:bo + 128], start=False, stop=True).then_inc(s["o"], 1)
                if on(i):
                    pe.wait_ge(s["q_st"], i + 1)
                    for g in range(G):
                        o_ = ps_6[:, g * K2:(g + 1) * K2]
                        nc.tensor.matmul(o_, wk_s[:, layer, g, :], xc_t[:, p, 128:128 + K2], start=True, stop=layer == 0)
                        if layer:
                            nc.tensor.matmul(o_, bias_bf[:, BK + g * 128:BK + (g + 1) * 128], ones_bf[:, 0:K2], start=False, stop=True)
                    o_ = ps_6[0:K2, G * K2:G * K2 + 128]
                    mm = nc.tensor.matmul(o_, xc_t[:, p, 128:128 + K2], wv_s[:, layer, :], start=True, stop=layer == 0)
                    if layer:
                        mm = nc.tensor.matmul(o_, ones_bf[:, 0:K2], bias_bf[:, BV:BV + 128], start=False, stop=True)
                    mm.then_inc(s["kv"], 1)
                if on(t):
                    pe.wait_ge(s["pe2"], t + 1)
                    pe.wait_ge(s["pe3"], t + 1)
                    for g in range(G):
                        for j in range(4):
                            mm = nc.tensor.matmul(ps_a[32 * j:32 * j + 32, g * 128:(g + 1) * 128], v_s[:, (b - 2) % TB, 4 * g + j, :],
                                                  pt_s[:, j, g, :], start=True, stop=True)
                    mm.then_inc(s["u"], 1)
                if layer:
                    for b_ in range(TB):
                        if due(r, b, 8 + b_):
                            router_hidden(pe, r - (8 + b_) // TB, b_)
                if on(i + 1):
                    if on(w):
                        pe.wait_ge(s["x_new"], w + 1)
                    next_transposes(pe, i + 1, 1 - p).then_inc(s["xct"], 1)
                if on(i - 1):
                    pe.wait_ge(s["sd"], i)
                for b_ in range(TB):
                    step = 9 + b_ if layer else 8
                    if due(r, b, step):
                        R = r - step // TB
                        if isinstance(R, int) and not on(i - 1):
                            wait(pe, z["lg"], R)
                        router_logits(pe, R, b_)
                if on(i):
                    pe.wait_ge(s["k_st"], i + 1)
                    if layer == 0:
                        pe.wait_ge(s["pen"], i + 1)
                    if due(r, b, CHAIN):
                        pe.wait_ge(z["lg"], r - CHAIN // TB + 1)
                    for j in range(4):
                        o_ = ps_s[:, j, 0:G * K2].rearrange("q (g k) -> q g k", g=G)
                        if layer == 0:
                            nc.tensor.matmul(o_, ident_bf[:, :], pen0[:, p:p + 1, :].broadcast_to([128, G, K2]), start=True, stop=True)
                        else:
                            nc.tensor.matmul(o_, ones_all[:, :], pen1[:, bass.ds(i - o, 1), :].broadcast_to([128, G, K2]), start=True, stop=True)
                    for g in range(G):
                        for j in range(4):
                            row = 32 * j
                            mm = nc.tensor.matmul(ps_s[:, j, g * K2:(g + 1) * K2], q_st[row:row + 32, g, :], k_st[row:row + 32, g, :],
                                                  start=False, stop=True, skip_group_check=True)
                    mm.then_inc(s["s"], 1)
                if due(r, b, 7):
                    if on(t):
                        pe.wait_ge(s["u_ev"], t + 1)
                    token_transposes(pe, r - 1)
                if due(r, b, PLACE - 1):
                    place(pe, r - (PLACE - 1) // TB, i)

            def pe_prog(pe):
                if layer == 0:
                    pe.wait_ge(m["setup_ld"], NLD)
                    pe.wait_ge(m["const_ok"], NCONST_OK)
                    pe.wait_ge(m["bias_ok"], BIAS_STEPS)
                else:
                    pe.wait_ge(m["pen_moved"], 48)
                    pe.wait_ge(m["phase_end"], 2 * 4)
                next_transposes(pe, o, 0).then_inc(s["xct"], 1)
                steps(pe, pe_step)
                phase_end(pe)

            def evacuate_transposes(act, i, p):
                act.wait_ge(s["xct"], xct_of(i))
                nc.scalar.activation(xc_t[:, p, :], ps_7[:, 0:128 + K2], ACT.Copy).then_inc(s["xct_ev"], 1)

            def router_relu(act, R, b):
                act.wait_ge(z["hid"], R * TB - o + b + 1)
                wait(act, z["h_lo"], R * TB - o + b)
                wait(act, z["l"], R * TB + b)
                for c in range(C):
                    ins = nc.scalar.activation(h32[:, c, 0:128], ps_b[:, c * 128:(c + 1) * 128], ACT.Relu, bias=rb1_f[:, c:c + 1])
                ins.then_inc(z["h_ev"], 1)
                act.wait_ge(z["h_ev"], R * TB - o + b + 1)
                nc.scalar.activation(hr_hl[:, 0], h32[:, :, 0:128], ACT.Copy).then_inc(z["h_hi"], 1)

            def load_weights(act, r):
                act.dma_start(stage[:, :], weights[layer, bass.ds(r - OR, 1), :, :].rearrange("e d n -> d (e n)")).then_inc(z["w_ld"], 16)

            def normalise_again(act, R):
                act.wait_ge(z["stat"], R - OR + 1)
                wait(act, z["sorted"], sorted_count(R))
                for b_ in range(TB):
                    ins = nc.scalar.activation(xc4[:, b_, :], token_rows(R, b_), ACT.Identity,
                                               bias=stat_all[:, bass.ds((R - OR) * TB + b_, 1), 0:1].rearrange("p b k -> p (b k)"))
                ins.then_inc(z["centred"], 1)
                act.wait_ge(z["centred"], R - OR + 1)
                for b_ in range(TB):
                    ins = nc.scalar.activation(xsc[:, b_, :], xc4[:, b_, :], ACT.Copy,
                                               scale=stat_all[:, bass.ds((R - OR) * TB + b_, 1), 1:2].rearrange("p b k -> p (b k)"))
                ins.then_inc(z["xsc"], 1)

            def act_step(act, r, b):
                i = r * TB + b
                if b == 0 and block_on(r):
                    act.wait_ge(z["w_ld"], 16 * (r + 1))
                    nc.scalar.activation(w_hl[:, 0, bass.ds(r - OR, 1), :].rearrange("d e n -> d (e n)"), stage[:, :], ACT.Copy).then_inc(z["w_hi"], 1)
                if b == 2 and block_on(r) and block_on(r + 1):
                    act.wait_ge(z["w_lo"], r + 1)
                    load_weights(act, r + 1)
                p = b % 2
                k, t, w = i - 1, i - 2, i - 3

                def evacuate(j):
                    act.wait_ge(s[f"pt{j}"], t + 1)
                    ps = (ps_a, ps_b)[j % 2]
                    nc.scalar.activation(pt_s[:, j, :, :].rearrange("k g q -> k (g q)"), ps[0:K2, :], ACT.Copy).then_inc(s[f"pe{j}"], 1)

                if due(r, b, 8):
                    act.wait_ge(z["xt"], r - 1)
                    nc.scalar.activation(xt_hl[:, 0, :], ps_a[:, :], ACT.Copy).then_inc(z["hi"], 1)
                if on(i):
                    act.wait_ge(s["q"], i + 1)
                    wait(act, s["q_st"], i)
                    nc.scalar.activation(q_hi[:, :, :].rearrange("p g q -> p (g q)"), ps_6[:, :], ACT.Copy).then_inc(s["q_hi"], 1)
                if on(t):
                    evacuate(0)
                    evacuate(1)
                if on(w):
                    act.wait_ge(s["a_t"], w + 1)
                    nc.scalar.activation(at[:, :], ps_7[:, 0:128], ACT.Copy).then_inc(s["at_ev"], 1)
                if on(t):
                    evacuate(2)
                    evacuate(3)
                if layer and due(r, b, SORT):
                    normalise_again(act, r - SORT // TB)
                if not layer and due(r, b, SORT):
                    R = r - SORT // TB
                    act.wait_ge(z["xn"], R + 1)
                    wait(act, z["sorted"], sorted_count(R))
                    nc.scalar.activation(xsc[:, :, :], xn4[:, :, :], ACT.Copy).then_inc(z["xsc"], 1)
                if on(i):
                    act.wait_ge(s["kv"], i + 1)
                    nc.scalar.activation(v_s[:, b, :, 0:HD], ps_6[0:K2, G * K2:G * K2 + 128].rearrange("k (h d) -> k h d", h=H),
                                         ACT.Copy).then_inc(s["v_ev"], 1)
                    wait(act, s["k_st"], i)
                    nc.scalar.activation(k_hi[:, :, :].rearrange("p g k -> p (g k)"), ps_6[:, 0:G * K2], ACT.Copy).then_inc(s["k_hi"], 1)
                if on(t):
                    act.wait_ge(s["u"], t + 1)
                    nc.scalar.activation(u_s[:, :, :].rearrange("p g q -> p (g q)"), ps_a[:, :], ACT.Copy).then_inc(s["u_ev"], 1)
                if on(i + 1):
                    evacuate_transposes(act, i + 1, 1 - p)
                if on(k):
                    act.wait_ge(s["sd"], k + 1)
                    nc.scalar.activation(p_s[:, :, :, :].rearrange("q j g k -> q (j g k)"), sd[:, :, :, :].rearrange("q j g k -> q (j g k)"),
                                         ACT.Exp).then_inc(s["p"], 1)
                if layer:
                    for b_ in range(TB):
                        if due(r, b, 8 + b_):
                            router_relu(act, r - (8 + b_) // TB, b_)
                if due(r, b, CHAIN):
                    act.wait_ge(z["sub"], r - CHAIN // TB + 1)
                    nc.scalar.activation(lg[:, :, :], lg[:, :, :], ACT.Exp).then_inc(z["exp"], 1)

            def act_prog(act):
                if layer == 0:
                    setup_act(act)
                    act.wait_ge(m["const_ok"], NCONST_OK)
                else:
                    act.wait_ge(m["phase_end"], 2 * 4)
                load_weights(act, OR)
                evacuate_transposes(act, o, 0)
                steps(act, act_step)
                phase_end(act)

            def norm_stats(dve, i, p):
                xb = x_all[:, bass.ds(i - o, 1), :].rearrange("s b d -> s (b d)")
                if layer == 0:
                    wait(dve, s[f"x_ld{p}"], loaded(i, p))
                elif isinstance(i, int):
                    dve.wait_ge(z["combined"], TOPK[0] * (i - o + 1))
                if isinstance(i, int):
                    wait(dve, s["xn"], i - 1)
                nc.vector.bn_stats(stats[:, p, :], xb).then_inc(s["st1"], 1)

            def norm_aggregate(p):
                nc.vector.bn_aggr(mv[:, p, :], stats[:, p, :]).then_inc(s["st2"], 1)

            def normalise(dve, i, p, n):
                wait(dve, s["st1"], n)
                wait(dve, s["st4"], i + 1)
                wait(dve, s["xct"], xct_of(i - 2))
                nc.vector.tensor_scalar(xn[:, p, :], x_all[:, bass.ds(i - o, 1), :].rearrange("s b d -> s (b d)"), mv[:, p, 0:1], rstd[:, p, :],
                                        ALU.subtract, ALU.mult).then_inc(s["xn"], 1)

            def router_logits_out(dve, R):
                dve.wait_ge(z["l"], R * TB + TB)
                nc.vector.tensor_copy(lg[:, :, :].rearrange("p b e -> p (b e)"), ps_s[:, 0, FREE + 128:FREE + 128 + TB * E]).then_inc(z["lg"], 1)

            def router_pick(dve, R):
                dve.wait_ge(z["lg"], R + 1)
                mine = lg[:, :, :].unsqueeze(3).broadcast_to([128, TB, E, E])
                other = lg[:, :, :].unsqueeze(2).broadcast_to([128, TB, E, E])
                nc.vector.tensor_tensor(cmp_a[:, :, :, :], other, mine, ALU.is_gt)
                nc.vector.tensor_tensor(cmp_b[:, :, :, :], other, mine, ALU.is_equal).then_inc(z["cmp"], 1)
                nc.vector.tensor_reduce(lmax[:, :], lg[:, :, :], AX, ALU.max).then_inc(z["lmax"], 1)
                dve.wait_ge(z["lmax"], R + 1)
                nc.vector.tensor_tensor(lg[:, :, :], lg[:, :, :], lmax[:, :].unsqueeze(2).broadcast_to([128, TB, E]), ALU.subtract).then_inc(z["sub"], 1)
                dve.wait_ge(z["cmp"], R + 1)
                low = cst[:, C_LOW:C_LOW + E * E].rearrange("p (a b) -> p a b", a=E).unsqueeze(1).broadcast_to([128, TB, E, E])
                nc.vector.tensor_tensor(cmp_b[:, :, :, :], cmp_b[:, :, :, :], low, ALU.mult).then_inc(z["cmq"], 1)
                dve.wait_ge(z["cmq"], R + 1)
                nc.vector.tensor_tensor(cmp_a[:, :, :, :], cmp_a[:, :, :, :], cmp_b[:, :, :, :], ALU.add).then_inc(z["cms"], 1)
                dve.wait_ge(z["cms"], R + 1)
                nc.vector.tensor_reduce(rank[:, :, :], cmp_a[:, :, :, :], AX, ALU.add).then_inc(z["rank"], 1)
                dve.wait_ge(z["rank"], R + 1)
                nc.vector.tensor_scalar(sel_bf[:, 0:TB, :], rank[:, :, :], float(K), None, ALU.is_lt).then_inc(z["sel"], 1)

            def router_gates(dve, R):
                dve.wait_ge(z["sel"], R + 1)
                dve.wait_ge(z["exp"], R + 1)
                nc.vector.tensor_tensor(lg[:, :, :], lg[:, :, :], sel_bf[:, 0:TB, :], ALU.mult).then_inc(z["prod"], 1)
                dve.wait_ge(z["prod"], R + 1)
                nc.vector.tensor_reduce(lsum[:, :], lg[:, :, :], AX, ALU.add).then_inc(z["sum"], 1)
                dve.wait_ge(z["sum"], R + 1)
                nc.vector.reciprocal(lsum[:, :], lsum[:, :]).then_inc(z["rec"], 1)
                dve.wait_ge(z["rec"], R + 1)
                nc.vector.scalar_tensor_tensor(gate[:, :, :], lg[:, :, :], tg[:, 2 + layer:3 + layer],
                                               lsum[:, :].unsqueeze(2).broadcast_to([128, TB, E]), ALU.mult, ALU.mult).then_inc(z["gate"], 1)

            def token_places(dve, R):
                dve.wait_ge(z["pos"], R + 1)
                dve.wait_ge(z["end"], R)
                nc.vector.tensor_tensor(pos[:, :, :], ps_7[:, 0:TB * E].rearrange("p (b e) -> p b e", b=TB),
                                        row_end[:, :].unsqueeze(1).broadcast_to([128, TB, E]), ALU.add).then_inc(z["pos_ev"], 1)
                dve.wait_ge(z["pos_ev"], R + 1)
                nc.vector.tensor_tensor(row_end[:, :], ps_7[:, TB * E:(TB + 1) * E], row_end[:, :], ALU.add).then_inc(z["end"], 1)

            def token_rows_and_gates(dve, R):
                shape = [128, TB, K, E]
                of_k = is_k[:, :, 0:K, :]
                nc.vector.tensor_tensor(of_k, rank[:, :, :].unsqueeze(2).broadcast_to(shape),
                                        cst[:, C_K:C_K + K * E].rearrange("p (k e) -> p k e", k=K).unsqueeze(1).broadcast_to(shape),
                                        ALU.is_equal).then_inc(z["is_k"], 1)
                dve.wait_ge(z["is_k"], R + 1)
                dve.wait_ge(z["end"], R + 1)
                dve.wait_ge(z["gate"], R + 1)
                nc.vector.tensor_tensor(pick[:, :, 0:K, :], of_k, pos[:, :, :].unsqueeze(2).broadcast_to(shape), ALU.mult)
                nc.vector.tensor_tensor(pick2[:, :, 0:K, :], of_k, gate[:, :, :].unsqueeze(2).broadcast_to(shape), ALU.mult).then_inc(z["pick"], 1)
                dve.wait_ge(z["pick"], R + 1)
                nc.vector.tensor_reduce(idx_f[:, :, 0:K], pick[:, :, 0:K, :], AX, ALU.add).then_inc(z["idx_f"], 1)
                nc.vector.tensor_reduce(gk_all[:, bass.ds((R - OR) * TB, TB), 0:K], pick2[:, :, 0:K, :], AX, ALU.add).then_inc(z["gk"], 1)
                dve.wait_ge(z["idx_f"], R + 1)
                wait(dve, z["sorted"], sorted_count(R))
                nc.vector.tensor_copy(row_all[:, bass.ds((R - OR) * TB, TB), 0:K], idx_f[:, :, 0:K])
                nc.vector.tensor_copy(idx4[:, :, 0:K], idx_f[:, :, 0:K]).then_inc(z["idx"], 1)

            def combine(dve, j, p, ks=range(TOPK[0])):
                xb = x_all[:, bass.ds(j - o, 1), :].rearrange("s b d -> s (b d)")
                for k in ks:
                    if k == 0:
                        dve.wait_ge(z[f"g_ld{p}"], 8 * TOPK[0] * (j - o - p) + 16 * TOPK[0])
                    wait(dve, z["combined"], TOPK[0] * (j - o) + k)
                    nc.vector.scalar_tensor_tensor(xb, yg[:, p * TOPK[0] + k, :], gk_all[:, bass.ds(j - o, 1), k:k + 1].rearrange("s b k -> s (b k)"),
                                                   xb, ALU.mult, ALU.add).then_inc(z["combined"], 1)

            def router_split(dve, R, b):
                dve.wait_ge(z["h_hi"], R * TB - o + b + 1)
                nc.vector.tensor_tensor(hr_hl[:, 1], h32[:, :, 0:128], hr_hl[:, 0], ALU.subtract).then_inc(z["h_lo"], 1)

            def dve_step(dve, r, b):
                i = r * TB + b
                p = b % 2
                k, w = i - 1, i - 3
                sc = ps_s[:, :, 0:G * K2].rearrange("q j (g k) -> q j g k", g=G)
                if due(r, b, PLACE):
                    token_places(dve, r - PLACE // TB)
                if on(k):
                    dve.wait_ge(s["s"], k + 1)
                    nc.vector.tensor_reduce(mx[:, :].rearrange("q (j g) -> q j g", j=4), sc, AX, ALU.max).then_inc(s["mx"], 1)
                if due(r, b, CHAIN):
                    router_logits_out(dve, r - CHAIN // TB)
                if on(w):
                    dve.wait_ge(s["ut"], w + 1)
                    ut = ps_7[:, :].rearrange("q (h r) -> q h r", r=32)
                    nc.vector.reciprocal(rden[:, :], ut[:, :, HD]).then_inc(s["rden"], 1)
                    dve.wait_ge(s["rden"], w + 1)
                    nc.vector.tensor_tensor(an[:, :, :], ut[:, :, 0:HD], rden[:, :].unsqueeze(2).broadcast_to([128, H, HD]),
                                            ALU.mult).then_inc(s["an"], 1)
                if due(r, b, 8):
                    dve.wait_ge(z["hi"], r - 1)
                    nc.vector.tensor_tensor(xt_hl[:, 1, :], ps_a[:, :], xt_hl[:, 0, :], ALU.subtract).then_inc(z["lo"], 1)
                if on(i):
                    wait(dve, s["xn"], i + 1)
                    if layer and on(i + 2):
                        dve.wait_ge(z["combined"], TOPK[0] * (i - o + 3))
                    dve.wait_ge(s["q_hi"], i + 1)
                    nc.vector.scalar_tensor_tensor(q_st[:, :, :].rearrange("p g q -> p (g q)"), q_hi[:, :, :].rearrange("p g q -> p (g q)"), neg_q,
                                                   ps_6[:, :], ALU.mult, ALU.add).then_inc(s["q_st"], 1)
                if on(k):
                    dve.wait_ge(s["mx"], k + 1)
                    wait(dve, s["p"], k)
                    nc.vector.tensor_tensor(sd[:, :, :, :], sc, mx[:, :].rearrange("q (j g) -> q j g", j=4).unsqueeze(3).broadcast_to([128, 4, G, K2]),
                                            ALU.subtract).then_inc(s["sd"], 1)
                if on(w):
                    dve.wait_ge(s["o"], w + 1)
                    xb = x_all[:, bass.ds(w - o, 1), :].rearrange("s b d -> s (b d)")
                    nc.vector.scalar_tensor_tensor(xb, ps_7[:, 0:128], tg[:, layer:layer + 1], xb, ALU.mult, ALU.add).then_inc(s["x_new"], 1)
                if on(i + 2):
                    norm_stats(dve, i + 2, p)
                if due(r, b, 6):
                    dve.wait_ge(s["x_new"], w + 1)
                if on(i + 1):
                    normalise(dve, i + 1, 1 - p, i + 3 if on(i + 2) else 0)
                if on(i + 2):
                    norm_aggregate(p)
                if due(r, b, 6):
                    for b_ in range(TB):
                        ins = nc.vector.bn_stats(st4[:, b_, :], token_rows(r - 1, b_))
                    ins.then_inc(z["st"], 1)
                if layer and on(i + 3):
                    combine(dve, i + 3, 1 - p, (0,))
                if layer:
                    for b_ in range(TB):
                        if due(r, b, 9 + b_):
                            router_split(dve, r - (9 + b_) // TB, b_)
                if layer and on(i + 3):
                    combine(dve, i + 3, 1 - p, (1,))
                if on(i):
                    dve.wait_ge(s["k_hi"], i + 1)
                    nc.vector.scalar_tensor_tensor(k_st[:, :, :].rearrange("p g k -> p (g k)"), k_hi[:, :, :].rearrange("p g k -> p (g k)"), neg_k,
                                                   ps_6[:, 0:G * K2], ALU.mult, ALU.add).then_inc(s["k_st"], 1)
                if due(r, b, 6):
                    dve.wait_ge(z["st"], r)
                    nc.vector.memset(junk[:, :], 0.0)
                    for b_ in range(TB):
                        ins = nc.vector.bn_aggr(mv4[:, b_, :], st4[:, b_, :])
                    ins.then_inc(z["st2"], 1)
                if due(r, b, 7):
                    dve.wait_ge(z["st4"], r)
                    if layer == 0:
                        wait(dve, z["xsc"], r - 1)
                    wait(dve, z["xt"], r - 1)
                    for b_ in range(TB):
                        ins = nc.vector.tensor_scalar(xn4[:, b_, :], token_rows(r - 1, b_), mv4[:, b_, 0:1], rs4[:, b_, :], ALU.subtract, ALU.mult)
                    ins.then_inc(z["xn"], 1)
                if layer and due(r, b, 7):
                    of_block = stat_all[:, bass.ds((r - 1 - OR) * TB, TB), :]
                    nc.vector.tensor_scalar(of_block[:, :, 0:1], mv4[:, :, 0:1], -1.0, None, ALU.mult)
                    nc.vector.tensor_copy(of_block[:, :, 1:2], rs4[:, :, :]).then_inc(z["stat"], 1)
                if b == 1 and block_on(r):
                    dve.wait_ge(z["w_hi"], r + 1)
                    wt = w_hl[:, :, bass.ds(r - OR, 1), :].rearrange("d t e n -> d t (e n)")
                    nc.vector.tensor_tensor(wt[:, 1], stage[:, :], wt[:, 0], ALU.subtract).then_inc(z["w_lo"], 1)
                if layer and on(i + 3):
                    combine(dve, i + 3, 1 - p, (2, 3))
                if due(r, b, CHAIN):
                    router_pick(dve, r - CHAIN // TB)
                if due(r, b, CHAIN + 1):
                    router_gates(dve, r - (CHAIN + 1) // TB)
                if due(r, b, PLACE):
                    token_rows_and_gates(dve, r - PLACE // TB)

            def dve_prog(dve):
                if layer == 0:
                    setup_dve(dve)
                    dve.wait_ge(m["const_ok"], NCONST_OK)
                else:
                    dve.wait_ge(m["phase_end"], 2 * 4)
                nc.vector.tensor_copy(row_end[:, :], cst[:, C_ROW0:C_ROW0 + E])
                if layer:
                    for j in range(3):
                        combine(dve, o + j, j % 2)
                norm_stats(dve, o, 0)
                norm_stats(dve, o + 1, 1)
                dve.wait_ge(s["st1"], o + 2)
                norm_aggregate(0)
                norm_aggregate(1)
                normalise(dve, o, 0, 0)
                steps(dve, dve_step)
                phase_end(dve)

            progs["sp"].append(sp_prog)
            progs["pool"].append(pool_prog)
            progs["pe"].append(pe_prog)
            progs["act"].append(act_prog)
            progs["dve"].append(dve_prog)

        def phase_end(eng):
            eng.drain().then_inc(m["phase_end"], 1)

        st4 = sb("st4", [128, TB, 6], F32)
        mv4 = sb("mv4", [128, TB, 2], F32)
        rs4 = sb("rs4", [128, TB, 1], F32)

        def experts(layer):
            o = layer * TILES[0]
            NT = TILES[layer]
            n = ("zeroed", "tab", "tab_ok", "xg_ld0", "xg_ld1", "xt", "x_hi", "x_lo", "y", "y_ev", "y_st")
            s = {k: shared_sem("f_" + k) for k in n}
            ups = [shared_sem(f"f_up{c}") for c in range(C)]
            evs = [shared_sem(f"f_ev{c}") for c in range(C)]
            his = [shared_sem(f"f_hi{c}") for c in range(C)]
            los = [shared_sem(f"f_lo{c}") for c in range(C)]
            base = (1 + 2 * layer) * 4

            def row_of(eng, u):
                return eng.value_load(tab_row[0:1, bass.ds(u - o, 1)], min_val=0, max_val=E * CAP - TOK)

            def experts_of(eng, u, count):
                return nc.values_load_multi_w_load_instructions(tab_e[0:1, bass.ds(u - o, count)], engines=(eng.engine,), min_val=0, max_val=E - 1)[1]

            def expert_of(eng, u):
                return eng.value_load(tab_e[0:1, bass.ds(u - o, 1)], min_val=0, max_val=E - 1)

            def sp_prog(sp):
                if layer:
                    sp.wait_ge(m["phase_end"], 2 * 4)
                sp.wait_ge(s["tab_ok"], layer + 1)
                for e in range(E):
                    end = sp.value_load(end_i[0:1, e:e + 1], min_val=0, max_val=E * CAP - TOK)
                    sp.dma_start(xs[bass.ds(end, TOK), :].rearrange("(p j) d -> p (j d)", p=128), zeros).then_inc(s["zeroed"], 16)
                sp.wait_ge(s["zeroed"], 16 * E * (layer + 1))
                sp.wait_ge(shared_sem("r_sorted"), 16 * TB * NBLK * sum(TOPK[0:layer + 1]))

                def load(u, p):
                    wait(sp, s["xt"], u - 1)
                    sp.dma_start(xg[:, p, :], xs[bass.ds(row_of(sp, u), TOK), :].rearrange("(p j) d -> p (j d)", p=128)).then_inc(s[f"xg_ld{p}"], 16)

                def store(u, p):
                    wait(sp, s["y_st"], 16 * u)
                    sp.wait_ge(s["y_ev"], u + 1)
                    sp.dma_start(ys[bass.ds((u - o) * TOK, TOK), :].rearrange("(p j) d -> p (j d)", p=128), y_s[:, p, :]).then_inc(s["y_st"], 16)

                load(o, 0)
                load(o + 1, 1)
                load(o + 2, 0)
                load(o + 3, 1)
                store(o, 0)
                with sp.Fori(o + 2, o + NT - 3, 2) as u:
                    load(u + 2, 0)
                    store(u - 1, 1)
                    load(u + 3, 1)
                    store(u, 0)
                for u in (o + NT - 3, o + NT - 2, o + NT - 1):
                    store(u, (u - o) % 2)

            def pe_prog(pe):
                pe.wait_ge(m["phase_end"], base)
                pe.wait_ge(s["tab_ok"], layer + 1)

                def transposes(u, p):
                    pe.wait_ge(s[f"xg_ld{p}"], loaded(u, p))
                    wait(pe, s["x_lo"], u)
                    for b in range(TB):
                        mm = nc.tensor.transpose(ps_6[:, b * 128:(b + 1) * 128], xg[:, p, b * 128:(b + 1) * 128], ident)
                    mm.then_inc(s["xt"], 1)

                def up_products(u, p, e):
                    pe.wait_ge(s["x_lo"], u + 1)
                    for c in range(C):
                        wait(pe, evs[c], u)
                        for k, (a, w) in enumerate(((0, 0), (1, 0), (0, 1))):
                            mm = nc.tensor.matmul(ps_s[:, c, :], up_hl[:, w, bass.ds(e, 1), c * 128:(c + 1) * 128].rearrange("p e n -> p (e n)"),
                                                  xt2[:, p, a, :], start=k == 0, stop=k == 2)
                        mm.then_inc(ups[c], 1)

                def down_products(u, p, e):
                    ps = (ps_a, ps_b)[p]
                    pe.wait_ge(los[C - 1], u + 1)
                    wait(pe, s["y_ev"], u - 1)
                    for b in range(TB):
                        o_ = ps[:, b * 128:(b + 1) * 128]
                        if layer:
                            nc.tensor.matmul(o_, ones_bf[:, :], bias_bf[:, bass.ds(e * D + B2, D)], start=True, stop=False)
                        for c in range(C):
                            for k, (a, w) in enumerate(((0, 0), (0, 1), (1, 0))):
                                mm = nc.tensor.matmul(o_, h_hl[:, p, a, c, b * 128:(b + 1) * 128],
                                                      down_hl[:, w, bass.ds(e, 1), c, :].rearrange("p e d -> p (e d)"),
                                                      start=not layer and c == 0 and k == 0, stop=c == C - 1 and k == 2)
                    mm.then_inc(s["y"], 1)

                def pair(u):
                    e0, e1, e2 = experts_of(pe, u, 3)
                    up_products(u + 1, 1, e1)
                    transposes(u + 2, 0)
                    down_products(u, 0, e0)
                    up_products(u + 2, 0, e2)
                    transposes(u + 3, 1)
                    down_products(u + 1, 1, e1)

                transposes(o, 0)
                up_products(o, 0, expert_of(pe, o))
                transposes(o + 1, 1)
                pair(o)
                with pe.Fori(o + 2, o + NT - 3, 2) as u:
                    pair(u)
                u = o + NT - 2
                e1 = expert_of(pe, u + 1)
                up_products(u + 1, 1, e1)
                down_products(u, 0, expert_of(pe, u))
                down_products(u + 1, 1, e1)
                phase_end(pe)

            def act_prog(act):
                act.wait_ge(m["phase_end"], base)
                act.wait_ge(s["tab_ok"], layer + 1)

                def tokens_hi(u, p):
                    act.wait_ge(s["xt"], u + 1)
                    wait(act, ups[C - 1], u - 1)
                    nc.scalar.activation(xt2[:, p, 0, :], ps_6[:, :], ACT.Copy).then_inc(s["x_hi"], 1)

                def hidden(u):
                    if layer:
                        e = expert_of(act, u)
                    for c in range(C):
                        act.wait_ge(ups[c], u + 1)
                        wait(act, los[c], u)
                        if layer:
                            nc.scalar.activation(h32[:, c, :], ps_s[:, c, :], ACT.Relu,
                                                 bias=b1_f[:, bass.ds(e, 1), c:c + 1].rearrange("p e c -> p (e c)")).then_inc(evs[c], 1)
                        else:
                            nc.scalar.activation(h32[:, c, :], ps_s[:, c, :], ACT.Gelu_apprx_tanh).then_inc(evs[c], 1)

                def output(u, p):
                    act.wait_ge(s["y"], u + 1)
                    wait(act, s["y_st"], 16 * (u - 1))
                    nc.scalar.activation(y_s[:, p, :], (ps_a, ps_b)[p][:, :], ACT.Copy).then_inc(s["y_ev"], 1)

                def pair(u):
                    hidden(u + 1)
                    tokens_hi(u + 2, 0)
                    output(u, 0)
                    hidden(u + 2)
                    tokens_hi(u + 3, 1)
                    output(u + 1, 1)

                tokens_hi(o, 0)
                hidden(o)
                tokens_hi(o + 1, 1)
                pair(o)
                with act.Fori(o + 2, o + NT - 3, 2) as u:
                    pair(u)
                hidden(o + NT - 1)
                output(o + NT - 2, 0)
                output(o + NT - 1, 1)
                phase_end(act)

            def pool_prog(pool):
                pool.wait_ge(m["phase_end"], base)
                phase_end(pool)

            def tile_table(dve):
                STEPS = 16
                count = [STEPS * layer]

                def chain(ins):
                    count[0] += 1
                    ins.then_inc(s["tab"], 1)
                    dve.wait_ge(s["tab"], count[0])

                row0 = cst[:, C_ROW0:C_ROW0 + E]
                NJ = B * S // TOK
                chain(nc.vector.tensor_tensor(t_cnt[:, :], row_end[:, :], row0, ALU.subtract))
                chain(nc.vector.tensor_tensor(t_gt[:, :, :], t_cnt[:, :].unsqueeze(2).broadcast_to([128, E, NJ]),
                                              cst[:, C_J:C_J + NJ].unsqueeze(1).broadcast_to([128, E, NJ]), ALU.is_gt))
                chain(nc.vector.tensor_reduce(t_n[:, :], t_gt[:, :, :], AX, ALU.add))
                chain(nc.vector.tensor_tensor(t_low[:, :, :], t_n[0:1, :].unsqueeze(1).broadcast_to([1, E, E]),
                                              cst[0:1, C_LOW:C_LOW + E * E].rearrange("p (a b) -> p a b", a=E), ALU.mult))
                nc.vector.tensor_reduce(t_last[:, :], t_n[0:1, :], AX, ALU.add)
                chain(nc.vector.tensor_reduce(t_first[:, :], t_low[:, :, :], AX, ALU.add))
                chain(nc.vector.tensor_scalar(t_last[:, :], t_last[:, :], -1.0, None, ALU.add))
                nc.vector.tensor_scalar(t_step[:, 1:E], t_n[:, 0:E - 1], -float(TOK), float(CAP), ALU.mult, ALU.add)
                chain(nc.vector.tensor_scalar(t_tau[:, :], cst[0:1, C_TAU:C_TAU + MAXT], t_last[:, 0:1], None, ALU.min))
                shape = [1, MAXT, E - 1]
                ge = t_ge[:, :, 1:E]
                chain(nc.vector.tensor_tensor(ge, t_tau[:, :].unsqueeze(2).broadcast_to(shape),
                                              t_first[:, 1:E].unsqueeze(1).broadcast_to(shape), ALU.is_ge))
                nc.vector.tensor_reduce(t_row[:, :], ge, AX, ALU.add)
                chain(nc.vector.tensor_tensor(t_mul[:, :, 1:E], ge, t_step[0:1, 1:E].unsqueeze(1).broadcast_to(shape), ALU.mult))
                nc.vector.tensor_copy(end_i[:, :], row_end[0:1, :])
                chain(nc.vector.tensor_copy(tab_e[:, :], t_row[:, :]))
                chain(nc.vector.tensor_reduce(t_row[:, :], t_mul[:, :, 1:E], AX, ALU.add))
                chain(nc.vector.scalar_tensor_tensor(t_row[:, :], t_tau[:, :], float(TOK), t_row[:, :], ALU.mult, ALU.add))
                nc.vector.tensor_copy(tab_row[:, :], t_row[:, :]).then_inc(s["tab_ok"], 1)
                dve.wait_ge(m["phase_end"], base)
                K = TOPK[layer]
                rows = row_all[:, :, 0:K]
                work = h32[:, :, :].rearrange("p c n -> p (c n)")[:, 0:B * K * (E - 1)].rearrange("p (b k e) -> p b k e", b=B, k=K)
                for k in range(K):
                    ins = nc.vector.tensor_tensor(work[:, :, k], rows[:, :, k:k + 1].broadcast_to([128, B, E - 1]),
                                                  row0[:, 1:E].unsqueeze(1).broadcast_to([128, B, E - 1]), ALU.is_ge)
                chain(ins)
                for k in range(K):
                    ins = nc.vector.tensor_tensor(work[:, :, k], work[:, :, k], t_step[:, 1:E].unsqueeze(1).broadcast_to([128, B, E - 1]), ALU.mult)
                chain(ins)
                chain(nc.vector.tensor_reduce(y_off[:, :, 0:K], work, AX, ALU.add))
                chain(nc.vector.tensor_tensor(idx_all[:, :, 0:K], rows, y_off[:, :, 0:K], ALU.subtract))
                assert count[0] == STEPS * (layer + 1)

            def dve_prog(dve):
                if layer == 0:
                    nc.vector.memset(zeros, 0.0)
                tile_table(dve)

                def tokens_lo(u, p):
                    dve.wait_ge(s["x_hi"], u + 1)
                    nc.vector.tensor_tensor(xt2[:, p, 1, :], ps_6[:, :], xt2[:, p, 0, :], ALU.subtract).then_inc(s["x_lo"], 1)

                def hidden(u, p):
                    for c in range(C):
                        dve.wait_ge(evs[c], u + 1)
                        if c == 0:
                            wait(dve, s["y"], u - 1)
                        nc.vector.tensor_copy(h_hl[:, p, 0, c, :], h32[:, c, :]).then_inc(his[c], 1)
                        dve.wait_ge(his[c], u + 1)
                        nc.vector.tensor_tensor(h_hl[:, p, 1, c, :], h32[:, c, :], h_hl[:, p, 0, c, :], ALU.subtract).then_inc(los[c], 1)

                def pair(u):
                    hidden(u + 1, 1)
                    tokens_lo(u + 2, 0)
                    hidden(u + 2, 0)
                    tokens_lo(u + 3, 1)

                tokens_lo(o, 0)
                hidden(o, 0)
                tokens_lo(o + 1, 1)
                pair(o)
                with dve.Fori(o + 2, o + NT - 3, 2) as u:
                    pair(u)
                hidden(o + NT - 1, 1)
                phase_end(dve)

            progs["sp"].append(sp_prog)
            progs["pool"].append(pool_prog)
            progs["pe"].append(pe_prog)
            progs["act"].append(act_prog)
            progs["dve"].append(dve_prog)

        def finish():
            K, NG = TOPK[1], 4
            yf = wide[:, TOK:TOK + NG * TB * K * D].rearrange("p (a d) -> p a d", d=D)
            ld = [shared_sem(f"e_ld{q}") for q in range(NG)]
            copied, summed = shared_sem("e_idx"), shared_sem("e_sum")

            def groups(eng, f):
                for g in range(NG):
                    f(eng, g, g)
                with eng.Fori(NG, B // TB - NG + 1, NG) as g:
                    for q in range(NG):
                        f(eng, g + q, q)

            def gather(pool, g, q):
                wait(pool, summed, K * TB * (g - NG + 1))
                carry_waits(4)
                nc.gpsimd.tensor_copy(idx_g[:, q * TB:(q + 1) * TB, 0:K], idx_all[:, bass.ds(g * TB, TB), 0:K]).then_inc(copied, 1)
                pool.wait_ge(copied, g + 1)
                carry_waits(5)
                for b in range(TB):
                    for k in range(K):
                        nc.gpsimd.indirect_dma_start(yf[:, (q * TB + b) * K + k, :], None, ys,
                                                     bass.IndirectOffsetOnAxis(ap=idx_g[:, q * TB + b, k:k + 1], axis=0)).then_inc(ld[q], 16)

            def combine(dve, g, q):
                dve.wait_ge(ld[q], (g - q) * (16 * TB * K // NG) + 16 * TB * K)
                for k in range(K):
                    wait(dve, summed, K * TB * g + TB * k)
                    for b in range(TB):
                        xb = x_all[:, bass.ds(g * TB + b, 1), :].rearrange("s b d -> s (b d)")
                        nc.vector.scalar_tensor_tensor(xb, yf[:, (q * TB + b) * K + k, :],
                                                       gk_all[:, bass.ds(g * TB + b, 1), k:k + 1].rearrange("s b k -> s (b k)"),
                                                       xb, ALU.mult, ALU.add).then_inc(summed, 1)

            def pool_prog(pool):
                pool.wait_ge(m["phase_end"], 4 * 4)
                pool.wait_ge(shared_sem("f_y_st"), 16 * sum(TILES))
                groups(pool, gather)

            def dve_prog(dve):
                dve.wait_ge(m["phase_end"], 4 * 4)
                groups(dve, combine)

            progs["pool"].append(pool_prog)
            progs["dve"].append(dve_prog)
            return summed, K

        for layer in range(2):
            attention(layer)
            experts(layer)

        summed, per_batch = finish()

        def store(sp):
            for k in range(8):
                sp.wait_ge(summed, 8 * (k + 1) * per_batch)
                sp.dma_start(out[k * 8:(k + 1) * 8].rearrange("b s d -> s b d"), x_all[:, k * 8:(k + 1) * 8, :]).then_inc(m["out_st"], 16)
            sp.wait_ge(m["out_st"], 128)

        @block.sync
        def _(sp):
            for f in progs["sp"]:
                f(sp)
            store(sp)

        @block.gpsimd
        def _(pool):
            for f in progs["pool"]:
                f(pool)

        @block.scalar
        def _(act):
            for f in progs["act"]:
                f(act)

        @block.vector
        def _(dve):
            for f in progs["dve"]:
                f(dve)

        @block.tensor
        def _(pe):
            for f in progs["pe"]:
                f(pe)


def kernel(**inputs):
    import numpy as np
    import concourse.bacc as bacc
    from concourse import mybir
    from concourse.bass_utils import run_bass_kernel_spmd

    a = {k: np.ascontiguousarray(v) for k, v in inputs.items()}

    def stack(w, rows):
        w = w.reshape((G, 4, 1, HD) + w.shape[1:])
        full = np.zeros((G, 4, 4, HD) + w.shape[4:], w.dtype)
        full[:, :, 0:3] = w
        return full.reshape((G * 128,) + w.shape[4:])

    def stacks(name):
        both = [stack(a[f"L{l}_xattn_{name}"], G).T.reshape(D, G, 128) for l in range(2)]
        return np.ascontiguousarray(np.stack(both, 1))

    def both_t(name):
        return np.ascontiguousarray(np.stack([a[f"L{l}_xattn_{name}"].T for l in range(2)], 1))

    bias = np.concatenate([
        stack(a["L1_xattn_bq"], 0), stack(a["L1_xattn_bk"], 0), a["L1_xattn_bv"], a["L1_xattn_bo"], a["L0_xattn_bo"],
        a["L1_ffn_b2"].reshape(-1), a["L1_ffn_rb2"]])
    row = np.arange(128)
    consts = np.zeros((128, NCONST), np.float32)
    consts[:, C_ID:C_ID + 128] = np.eye(128)
    consts[:, C_NQ] = np.where(row // HD % 4 == 2, -1, 0)
    consts[:, C_NK] = np.where(row // HD % 4 == 1, -1, 0)
    consts[0:3, C_SEL:C_SEL + 3] = np.eye(3)
    consts[:, C_HALF:C_HALF + TB] = -0.5
    consts[:, C_EPS:C_EPS + TB] = EPS
    consts[:, C_TRI:C_TRI + 128] = np.triu(np.ones((128, 128)), 1)
    consts[:, C_K:C_K + TOPK[0] * E] = np.repeat(np.arange(TOPK[0]), E)
    consts[:, C_J:C_J + B * S // TOK] = np.arange(B * S // TOK) * TOK
    consts[:, C_TAU:C_TAU + MAXT] = np.arange(MAXT)
    consts[:, C_ROW0:C_ROW0 + E] = np.arange(E) * CAP
    consts[:, C_LOW:C_LOW + 64] = np.tril(np.ones((E, E)), -1).reshape(-1)
    small = np.concatenate([
        a["L0_ffn_router_w"], a["L1_ffn_rw1"], a["L1_ffn_rw2"].reshape(C, 128, E).transpose(1, 0, 2).reshape(128, -1),
        a["L1_ffn_b1"].reshape(E, C, 128).transpose(2, 0, 1).reshape(128, -1), a["L1_ffn_rb1"].reshape(C, 128).T], 1)
    up = [a["L0_ffn_up_w"], a["L1_ffn_W1"]]
    down = [a[n].reshape(E, C, 128, D).transpose(0, 2, 1, 3).reshape(E, 128, C * D) for n in ("L0_ffn_down_w", "L1_ffn_W2")]
    weights = np.stack([np.concatenate([up[l], down[l]]) for l in range(2)])
    arrays = {
        "x": a["x"], "ctx": a["ctx_1024"], "mask0": a["mask_Bx1xSxS2_if1"], "mask1": a["mask_BxS2_ff1"],
        "gates": np.concatenate([a["g_xattn"], a["g_ffn"]]), "consts": consts,
        "wq": stacks("Wq"), "wk": stacks("Wk"), "wv": both_t("Wv"), "wo": both_t("Wo"),
        "biases": np.ascontiguousarray(np.broadcast_to(bias, (3, NBIAS))), "small": small,
        "weights": np.ascontiguousarray(weights),
    }
    nc = bacc.Bacc("TRN2", target_bir_lowering=False, num_devices=1)
    t = {k: nc.dram_tensor(f"in_{k}", v.shape, mybir.dt.from_np(v.dtype), kind="ExternalInput").ap() for k, v in arrays.items()}
    out = nc.dram_tensor("out_0", (B, S, D), mybir.dt.float32, kind="ExternalOutput").ap()
    xs, ys = (nc.dram_tensor(n, (rows, D), mybir.dt.float32, kind="Internal").ap()
              for n, rows in (("sorted_x", E * CAP), ("sorted_y", MAXT * TOK)))
    flamingo(nc, t["x"], t["ctx"], t["mask0"], t["mask1"], t["gates"], t["consts"], t["wq"], t["wk"], t["wv"], t["wo"],
             t["biases"], t["small"], t["weights"], out, xs, ys)
    r = run_bass_kernel_spmd(nc, [{f"in_{k}": np.ascontiguousarray(v) for k, v in arrays.items()}], core_ids=[0])
    return r.results[0]["out_0"]
```
